# Optimizing a Trainium2 kernel written in Bass

```python
import numpy as np
import jax
import jax.numpy as jnp

def _softmax(x, axis=-1):
    return jax.nn.softmax(x, axis=axis)

def _gelu(x):
    return jax.nn.gelu(x, approximate=True)

def _silu(x):
    return jax.nn.silu(x)

def _sigmoid(x):
    return jax.nn.sigmoid(x)

def _layernorm(x, axis=-1, eps=1e-05):
    m = jnp.mean(x, axis=axis, keepdims=True)
    v = jnp.var(x, axis=axis, keepdims=True)
    return (x - m) / jnp.sqrt(v + eps)

def _scatter_add(tgt, idx, src, axis=0):
    return tgt.at[idx].add(src)

def _segment_sum(src, seg, n):
    return jax.ops.segment_sum(src, seg, n)
kernel_name = 'mk_recurrent_d1_jaxref_r8_937da6'

def setup_inputs(seed: int=0):
    np.random.seed(seed)
    _w = jnp.asarray

    def _L0_attn_setup():
        import jax, jax.numpy as jnp
        import numpy as np
        D_INNER, D_STATE, DT_RANK = (128, 16, 32)

        def _selective_scan(x, x_proj_w, dt_proj_w, dt_proj_b, A_log, Dp):
            A = -jnp.exp(A_log)
            dbc = jnp.einsum('bld,nd->bln', x, x_proj_w)
            delta, Bm, Cm = jnp.split(dbc, [DT_RANK, DT_RANK + D_STATE], axis=-1)
            delta = jax.nn.softplus(jnp.einsum('blr,dr->bld', delta, dt_proj_w) + dt_proj_b)
            deltaA = jnp.exp(delta[..., None] * A)
            BX = delta[..., None] * Bm[:, :, None, :] * x[..., None]

            def comb(e1, e2):
                a1, b1 = e1
                a2, b2 = e2
                return (a2 * a1, a2 * b1 + b2)
            _, hs = jax.lax.associative_scan(comb, (deltaA, BX), axis=1)
            y = jnp.einsum('blds,bls->bld', hs, Cm)
            return y + Dp * x
        key = jax.random.key(seed)
        ks = jax.random.split(key, 12)
        B, L = (4, 256)
        A_row = jnp.log(jnp.arange(1, D_STATE + 1, dtype=jnp.float32))
        A_log = jnp.tile(A_row[None, :], (D_INNER, 1))
        s = 0.02
        return {'x': jax.random.normal(ks[0], (B, L, D_INNER), jnp.float32), 'x_proj_w': jax.random.normal(ks[1], (DT_RANK + 2 * D_STATE, D_INNER), jnp.float32) * s, 'dt_proj_w': jax.random.normal(ks[2], (D_INNER, DT_RANK), jnp.float32) * DT_RANK ** (-0.5), 'dt_proj_b': jax.random.normal(ks[3], (D_INNER,), jnp.float32) * 0.1 - 4.0, 'A_log': A_log, 'D': jnp.ones((D_INNER,), jnp.float32), 'x_proj_b_w': jax.random.normal(ks[4], (DT_RANK + 2 * D_STATE, D_INNER), jnp.float32) * s, 'dt_proj_b_w': jax.random.normal(ks[5], (D_INNER, DT_RANK), jnp.float32) * DT_RANK ** (-0.5), 'dt_proj_b_b': jax.random.normal(ks[6], (D_INNER,), jnp.float32) * 0.1 - 4.0, 'A_b_log': A_log, 'D_b': jnp.ones((D_INNER,), jnp.float32)}
    _L0_attn_in = _L0_attn_setup()

    def _L0_ffn_setup():
        import jax, jax.numpy as jnp
        import numpy as np
        import math
        D_IN = 128
        FEATURES = (512, 512, 128)
        BATCH, SEQ = (8, 256)

        def _conn_dense(kernel_bool, x):
            w = jnp.where(kernel_bool, jnp.float32(1.0), jnp.float32(-1.0))
            return x @ w
        key = jax.random.key(seed)
        kx, kk0, kk1, kk2 = jax.random.split(key, 4)
        x = jax.random.normal(kx, (BATCH, SEQ, D_IN), dtype=jnp.float32)
        k0 = jax.random.randint(kk0, (2 * D_IN, FEATURES[0]), 0, 2).astype(jnp.bool_)
        k1 = jax.random.randint(kk1, (FEATURES[0], FEATURES[1]), 0, 2).astype(jnp.bool_)
        k2 = jax.random.randint(kk2, (FEATURES[1], FEATURES[2]), 0, 2).astype(jnp.bool_)
        s0 = jnp.asarray(1.0 / math.sqrt(2 * D_IN), dtype=jnp.float32)
        s1 = jnp.asarray(1.0 / math.sqrt(FEATURES[0]), dtype=jnp.float32)
        s2 = jnp.asarray(1.0 / math.sqrt(FEATURES[1]), dtype=jnp.float32)
        return {'x': x, 'k0': k0, 'k1': k1, 'k2': k2, 's0': s0, 's1': s1, 's2': s2}
    _L0_ffn_in = _L0_ffn_setup()
    _d = {'L0_attn_x': _L0_attn_in['x'], 'L0_attn_x_proj_w': _L0_attn_in['x_proj_w'], 'L0_attn_dt_proj_w': _L0_attn_in['dt_proj_w'], 'L0_attn_dt_proj_b': _L0_attn_in['dt_proj_b'], 'L0_attn_A_log': _L0_attn_in['A_log'], 'L0_attn_D': _L0_attn_in['D'], 'L0_attn_x_proj_b_w': _L0_attn_in['x_proj_b_w'], 'L0_attn_dt_proj_b_w': _L0_attn_in['dt_proj_b_w'], 'L0_attn_dt_proj_b_b': _L0_attn_in['dt_proj_b_b'], 'L0_attn_A_b_log': _L0_attn_in['A_b_log'], 'L0_attn_D_b': _L0_attn_in['D_b'], 'L0_ffn_k0': _L0_ffn_in['k0'], 'L0_ffn_k1': _L0_ffn_in['k1'], 'L0_ffn_k2': _L0_ffn_in['k2'], 'L0_ffn_s0': _L0_ffn_in['s0'], 'L0_ffn_s1': _L0_ffn_in['s1'], 'L0_ffn_s2': _L0_ffn_in['s2']}
    _x0 = _d['L0_attn_x']
    _d['L0_attn_x'] = jax.random.normal(jax.random.fold_in(jax.random.key(seed), 1), (8, 1024, 128), dtype=_x0.dtype)
    del _x0
    return _d

def reference(L0_attn_x, L0_attn_x_proj_w, L0_attn_dt_proj_w, L0_attn_dt_proj_b, L0_attn_A_log, L0_attn_D, L0_attn_x_proj_b_w, L0_attn_dt_proj_b_w, L0_attn_dt_proj_b_b, L0_attn_A_b_log, L0_attn_D_b, L0_ffn_k0, L0_ffn_k1, L0_ffn_k2, L0_ffn_s0, L0_ffn_s1, L0_ffn_s2):

    def _L0_attn_ref(x, x_proj_w, dt_proj_w, dt_proj_b, A_log, D, x_proj_b_w, dt_proj_b_w, dt_proj_b_b, A_b_log, D_b):
        import jax, jax.numpy as jnp
        import numpy as np
        D_INNER, D_STATE, DT_RANK = (128, 16, 32)

        def _selective_scan(x, x_proj_w, dt_proj_w, dt_proj_b, A_log, Dp):
            A = -jnp.exp(A_log)
            dbc = jnp.einsum('bld,nd->bln', x, x_proj_w)
            delta, Bm, Cm = jnp.split(dbc, [DT_RANK, DT_RANK + D_STATE], axis=-1)
            delta = jax.nn.softplus(jnp.einsum('blr,dr->bld', delta, dt_proj_w) + dt_proj_b)
            deltaA = jnp.exp(delta[..., None] * A)
            BX = delta[..., None] * Bm[:, :, None, :] * x[..., None]

            def comb(e1, e2):
                a1, b1 = e1
                a2, b2 = e2
                return (a2 * a1, a2 * b1 + b2)
            _, hs = jax.lax.associative_scan(comb, (deltaA, BX), axis=1)
            y = jnp.einsum('blds,bls->bld', hs, Cm)
            return y + Dp * x
        y = _selective_scan(x, x_proj_w, dt_proj_w, dt_proj_b, A_log, D)
        xb = x[:, ::-1]
        yb = _selective_scan(xb, x_proj_b_w, dt_proj_b_w, dt_proj_b_b, A_b_log, D_b)
        return y + yb[:, ::-1]

    def _L0_ffn_ref(x, k0, k1, k2, s0, s1, s2):
        import jax, jax.numpy as jnp
        import numpy as np
        import math
        D_IN = 128
        FEATURES = (512, 512, 128)
        BATCH, SEQ = (8, 256)

        def _conn_dense(kernel_bool, x):
            w = jnp.where(kernel_bool, jnp.float32(1.0), jnp.float32(-1.0))
            return x @ w
        h = jnp.concatenate([x, -x], axis=-1)
        h = s0 * _conn_dense(k0, h)
        h = jax.nn.relu(h) * 2
        h = s1 * _conn_dense(k1, h)
        h = jax.nn.relu(h) * 2
        h = s2 * _conn_dense(k2, h)
        return h
    x = L0_attn_x
    xn = _layernorm(x, axis=-1)
    s = _L0_attn_ref(xn, L0_attn_x_proj_w, L0_attn_dt_proj_w, L0_attn_dt_proj_b, L0_attn_A_log, L0_attn_D, L0_attn_x_proj_b_w, L0_attn_dt_proj_b_w, L0_attn_dt_proj_b_b, L0_attn_A_b_log, L0_attn_D_b)
    g = _silu(_L0_ffn_ref(xn, L0_ffn_k0, L0_ffn_k1, L0_ffn_k2, L0_ffn_s0, L0_ffn_s1, L0_ffn_s2))
    x = x + s * g
    return x

_drawn_inputs = setup_inputs


def setup_inputs(seed=0):
    import zlib

    import numpy as np

    out = dict(_drawn_inputs(seed))
    spreads = {'L0_attn_D': (1.0, 0.2), 'L0_attn_D_b': (1.0, 0.2)}
    factors = {'L0_attn_x_proj_w': 8.0,
     'L0_attn_dt_proj_w': 8.0,
     'L0_attn_dt_proj_b': 8.0,
     'L0_attn_A_log': 8.0,
     'L0_attn_x_proj_b_w': 8.0,
     'L0_attn_dt_proj_b_w': 8.0,
     'L0_attn_dt_proj_b_b': 8.0,
     'L0_attn_A_b_log': 8.0}
    for name, (base, spread) in spreads.items():
        noise = np.random.default_rng([zlib.crc32(name.encode()), seed]).standard_normal(out[name].shape)
        drawn = base * np.exp(spread * noise) if base else spread * noise
        out[name] = jnp.asarray(drawn.astype(out[name].dtype))
    for name, factor in factors.items():
        out[name] = (out[name] * factor).astype(out[name].dtype)
    return out
```

```python
from contextlib import ExitStack

import concourse.bass as bass
from concourse import mybir

F32 = mybir.dt.float32
F32R = mybir.dt.float32r
U8 = mybir.dt.uint8
ALU = mybir.AluOpType
ACT = mybir.ActivationFunctionType

P = 128
BANK = 512
EPS = 1e-5
LOG_SLACK = 7e-8


def after(eng, sem, count):
    if isinstance(count, int) and count <= 0:
        return
    eng.wait_ge(sem, count)


def build_scan_and_gate(nc, x, x_proj, dt_proj, dt_bias, A_log, D_skip, k0, k1, k2, scales, out):
    NB, L, D = x.shape
    S = A_log[0].shape[1]
    R = dt_proj[0].shape[1]
    F = k0.shape[1]
    CH = P // S
    GROUPS = D // CH
    UNITS = 2 * GROUPS
    HALVES = L // BANK
    TILES = L // P
    TH = TILES // HALVES
    FM = F // P
    QUADS = 4
    Q = P // QUADS
    PER_Q = GROUPS // QUADS
    NH = 4
    NCG = 8
    LEAD = 5
    assert D == P and F == BANK and HALVES == 2 and GROUPS == 16 and UNITS % NCG == 0

    def group(k):
        return PER_Q * (k % QUADS) + k // QUADS

    LATE = [(UNITS + 0, "net0", 0, 0), (UNITS + 0, "net0", 1, 0), (UNITS + 1, "net0", 2, 0),
            (UNITS + 1, "net0", 3, 0), (UNITS + 2, "delta", 1, 0), (UNITS + 2, "delta", 1, 1),
            (UNITS + 4, "net1", 0, 0), (UNITS + 4, "net1", 1, 0)]
    FINISH = [(UNITS + 4, "store", 0, 0), (UNITS + 4, "store", 0, 1)]
    NET = [(7, "net1", 2, 0), (9, "net1", 3, 0), (10, "net0", 0, 1), (10, "net0", 1, 1),
           (11, "net0", 2, 1), (11, "net0", 3, 1), (13, "net2", 0, 0), (20, "net1", 0, 1),
           (22, "net1", 1, 1), (25, "net1", 2, 1), (27, "net1", 3, 1), (29, "net2", 0, 1)]
    BACK = [(6, "B", 1, 0), (6, "B", 1, 1), (8, "C", 1, 0), (8, "C", 1, 1)]
    NEXT = [(17, "turn", 0, 0), (17, "turn", 0, 1), (18, "delta", 0, 0), (18, "delta", 0, 1),
            (23, "B", 0, 0), (23, "B", 0, 1), (24, "C", 0, 0), (24, "C", 0, 1)]
    body = sorted(NET + BACK + NEXT + FINISH + LATE, key=lambda s: s[0])
    start = NEXT + LATE
    end = sorted(NET + BACK + FINISH, key=lambda s: s[0])
    SETUP = 3

    with ExitStack() as ctx:
        def sb(name, shape, dt=F32):
            return ctx.enter_context(nc.sbuf_tensor(name, shape, dt))

        def sem(name):
            return ctx.enter_context(nc.semaphore(name))

        ident = sb("ident", [P, P])
        spread = sb("spread", [P, GROUPS // 2, P], F32R)
        gather = sb("gather", [P, PER_Q, Q])
        skip_diag = sb("skip_diag", [P, P])
        w0 = sb("w0", [P, F])
        w1 = sb("w1", [P, FM, F])
        w2 = sb("w2", [P, FM, D])
        k0_sb = sb("k0_sb", [P, 2, F], U8)
        k1_sb = sb("k1_sb", [P, FM, F], U8)
        k2_sb = sb("k2_sb", [P, FM, D], U8)
        xp_sb = sb("xp_sb", [R + 2 * S, 2, D])
        dt_sb = sb("dt_sb", [D, 2, R])
        dtT = sb("dtT", [R, 2, D])
        w_delta = sb("w_delta", [D, 2, D])
        w_B = sb("w_B", [D, 2, P])
        w_C = sb("w_C", [D, 2, P])
        neg_A = sb("neg_A", [P, 2, GROUPS])
        a_nat = sb("a_nat", [GROUPS, 2, P])
        a_in = sb("a_in", [P, 2, GROUPS])
        bias_dt = sb("bias_dt", [D, 2])
        skips = sb("skips", [D, 3])
        s_in = sb("s_in", [P, 3])
        s_net = sb("s_net", [P, 3])
        eps = sb("eps", [P, 1])
        x_in = sb("x_in", [P, TILES, D])
        x_res = sb("x_res", [P, TILES, D])
        xnT = sb("xnT", [D, L])
        stats = sb("stats", [P, TILES, 6])
        moments = sb("moments", [P, TILES, 2])
        std = sb("std", [P, TILES])
        rstd = sb("rstd", [P, TILES])
        h1 = sb("h1", [P, FM, BANK])
        h2 = sb("h2", [P, FM, BANK])
        gate = sb("gate", [D, L])
        gated = sb("gated", [D, L])
        x_out = sb("x_out", [P, TILES, D])
        ez = sb("ez", [D, L])
        small = sb("small", [D, L])
        delta = sb("delta", [D, L])
        pos = sb("pos", [D, L])
        hi = [sb("delta_hi", [D, L], F32R), sb("u_hi", [D, L], F32R)]
        lo = [sb("delta_lo", [D, L], F32R), sb("u_lo", [D, L], F32R)]
        stack = [[sb(f"{n}_stack{d}", [P, 2, L], F32R) for n in ("delta", "u")] for d in range(2)]
        B_rep = [sb(f"B_rep{d}", [P, L]) for d in range(2)]
        C_rep = [sb(f"C_rep{d}", [P, L]) for d in range(2)]
        a = sb("a", [P, 2, L])
        h = sb("h", [P, NH, L])
        ch = sb("ch", [P, NCG, L])

        d_rep = ctx.enter_context(nc.psum_tensor("d_rep", [P, L], F32))
        u_rep = ctx.enter_context(nc.psum_tensor("u_rep", [P, L], F32))
        y = ctx.enter_context(nc.psum_tensor("y", [P, L], F32))
        work = [ctx.enter_context(nc.psum_tensor(f"work{n}", [P, BANK], F32)) for n in range(2)]

        small_loaded = sem("small_loaded")
        nets_loaded = sem("nets_loaded")
        x_loaded = sem("x_loaded")
        moved = sem("moved")
        ident_zero = sem("ident_zero")
        ident_ready = sem("ident_ready")
        spread_zero = sem("spread_zero")
        spread_built = sem("spread_built")
        gather_ones = sem("gather_ones")
        gather_cut = sem("gather_cut")
        gather_ready = sem("gather_ready")
        const_ready = sem("const_ready")
        dve_step = sem("dve_step")
        act_step = sem("act_step")
        work_full = [sem(f"work_full{n}") for n in range(2)]
        setup_taken = [sem(f"setup_taken{n}") for n in range(2)]
        moments_ready = sem("moments_ready")
        stats_ready = sem("stats_ready")
        std_ready = sem("std_ready")
        rstd_ready = sem("rstd_ready")
        xn_ready = sem("xn_ready")
        xnT_ready = sem("xnT_ready")
        z_taken = sem("z_taken")
        e_ready = sem("e_ready")
        ln_ready = sem("ln_ready")
        slope_ready = sem("slope_ready")
        small_ready = sem("small_ready")
        log1p_ready = sem("log1p_ready")
        delta_ready = sem("delta_ready")
        u_ready = sem("u_ready")
        hi_ready = [sem("delta_hi_ready"), sem("u_hi_ready")]
        lo_ready = [sem("delta_lo_ready"), sem("u_lo_ready")]
        stacked = [sem("delta_stacked"), sem("u_stacked")]
        B_ready = sem("B_ready")
        C_ready = sem("C_ready")
        h1_ready = sem("h1_ready")
        h2_ready = sem("h2_ready")
        gate_ready = sem("gate_ready")
        d_rep_ready = sem("d_rep_ready")
        a_ready = sem("a_ready")
        u_rep_ready = sem("u_rep_ready")
        bx_ready = sem("bx_ready")
        h_ready = sem("h_ready")
        ch_ready = sem("ch_ready")
        summed = sem("summed")
        gated_ready = sem("gated_ready")
        out_ready = sem("out_ready")

        def cols(half):
            return slice(half * BANK, (half + 1) * BANK)

        def batch_of(i, s, step, arg):
            if step == "store":
                return i
            return i + 1 if s >= UNITS or step == "turn" or (step in ("delta", "B", "C") and arg == 0) else i

        def taken(i, s, step, arg, half):
            b = batch_of(i, s, step, arg)
            if step in ("net0", "net1"):
                return (h1_ready if step == "net0" else h2_ready), FM * (HALVES * b + half) + arg + 1
            if step in ("delta", "B", "C"):
                return {"delta": z_taken, "B": B_ready, "C": C_ready}[step], HALVES * (2 * b + arg) + half + 1
            return {"turn": xnT_ready, "net2": gate_ready, "store": out_ready}[step], HALVES * b + half + 1

        class Section:

            def __init__(self, steps, first, per_batch=0):
                self.steps, self.first, self.per_batch = steps, first, per_batch

            def at(self, unit, i):
                for p, (s, step, arg, half) in enumerate(self.steps):
                    if s == unit:
                        n = self.first + p
                        yield batch_of(i, s, step, arg), step, arg, half, n % 2, n // 2 + i * (self.per_batch // 2), p

        assert len(body) % 2 == 0
        opening = Section(start, SETUP)
        looped = Section(body, SETUP + len(start), len(body))
        closing = Section(end, SETUP + len(start) + (NB - 1) * len(body))

        block = ctx.enter_context(nc.Block())

        @block.sync
        def _(sp):
            def load_x(b):
                after(sp, xnT_ready, HALVES * b)
                sp.dma_start(x_in[:], x[b].rearrange("(j p) d -> p j d", p=P)).then_inc(x_loaded, 16)

            def load_residual(b):
                sp.dma_start(x_res[:], x[b].rearrange("(j p) d -> p j d", p=P)).then_inc(moved, 16)

            def stack_parts(b, d):
                for n in range(2):
                    after(sp, hi_ready[n], 2 * b + d + 1)
                    after(sp, lo_ready[n], 2 * b + d + 1)
                    for t in range(2):
                        rows = slice(t * P // 2, (t + 1) * P // 2)
                        sp.dma_start(stack[d][n][0:P // 2, t, :].bitcast(F32), hi[n][rows, :].bitcast(F32))\
                            .then_inc(stacked[n], 16)
                        sp.dma_start(stack[d][n][P // 2:P, t, :].bitcast(F32), lo[n][rows, :].bitcast(F32))\
                            .then_inc(stacked[n], 16)

            def store(b):
                for half in range(HALVES):
                    after(sp, out_ready, HALVES * b + half + 1)
                    sp.dma_start(out[b, half * BANK:(half + 1) * BANK, :].rearrange("(j p) d -> p j d", p=P),
                                 x_out[:, half * TH:(half + 1) * TH, :]).then_inc(moved, 16)

            load_x(0)
            for d in range(2):
                sp.dma_start(xp_sb[:, d, :], x_proj[d]).then_inc(small_loaded, 16)
                sp.dma_start(dt_sb[:, d, :], dt_proj[d]).then_inc(small_loaded, 16)
                sp.dma_start(bias_dt[:, d:d + 1], dt_bias[d].rearrange("(p a) -> p a", a=1)).then_inc(small_loaded, 16)
                sp.dma_start(skips[:, d:d + 1], D_skip[d].rearrange("(p a) -> p a", a=1)).then_inc(small_loaded, 16)
                sp.dma_start(a_nat[:, d, :], A_log[d].rearrange("(g c) s -> g (c s)", c=CH)).then_inc(small_loaded, 16)
            for n in range(3):
                sp.dma_start(s_in[:, n:n + 1], scales[n].partition_broadcast(P)).then_inc(small_loaded, 16)
            sp.dma_start(k0_sb[:], k0.rearrange("(t p) n -> p t n", p=P)).then_inc(nets_loaded, 16)
            sp.dma_start(k1_sb[:], k1.rearrange("(t p) n -> p t n", p=P)).then_inc(nets_loaded, 16)
            sp.dma_start(k2_sb[:], k2.rearrange("(t p) n -> p t n", p=P)).then_inc(nets_loaded, 16)
            stack_parts(0, 0)
            with sp.Fori(0, NB - 1) as i:
                load_x(i + 1)
                stack_parts(i, 1)
                load_residual(i)
                stack_parts(i + 1, 0)
                store(i)
            stack_parts(NB - 1, 1)
            load_residual(NB - 1)
            store(NB - 1)
            sp.wait_ge(moved, 16 * (1 + HALVES) * NB)

        @block.gpsimd
        def _(pool):
            pool.memset(ident[:], 0.0).then_inc(ident_zero, 1)
            pool.wait_ge(ident_zero, 1)
            pool.affine_select(out=ident[:], in_=ident[:], compare_op=ALU.not_equal, fill=1.0, base=0,
                               pattern=[[-1, P]], channel_multiplier=1).then_inc(ident_ready, 1)
            flat = a[:, 0, :]
            pool.memset(flat, 0.0).then_inc(spread_zero, 1)
            for n in range(2):
                pool.wait_ge(spread_zero, n + 1)
                pool.affine_select(out=flat.rearrange("p (g c s) -> p g c s", g=GROUPS // 2, s=S),
                                   in_=flat.rearrange("p (g c s) -> p g c s", g=GROUPS // 2, s=S),
                                   compare_op=ALU.not_equal, fill=1.0, base=-n * P // 2,
                                   pattern=[[-CH, GROUPS // 2], [-1, CH], [0, S]],
                                   channel_multiplier=1).then_inc(spread_built if n else spread_zero, 1)
            pool.memset(gather[:], 1.0).then_inc(gather_ones, 1)
            pool.wait_ge(gather_ones, 1)
            pool.affine_select(out=gather[:], in_=gather[:], compare_op=ALU.is_ge, fill=0.0, base=0,
                               pattern=[[S * CH, PER_Q], [-S, Q]], channel_multiplier=1).then_inc(gather_cut, 1)
            pool.wait_ge(gather_cut, 1)
            pool.affine_select(out=gather[:], in_=gather[:], compare_op=ALU.is_ge, fill=0.0, base=S - 1,
                               pattern=[[-S * CH, PER_Q], [S, Q]], channel_multiplier=-1).then_inc(gather_ready, 1)

            def normalise():
                for j in range(TILES):
                    last = pool.tensor_scalar(x_in[:, j, :], x_in[:, j, :], moments[:, j, 0:1], rstd[:, j:j + 1],
                                              ALU.subtract, ALU.mult)
                last.then_inc(xn_ready, 1)

            def small_log1p(phase):
                pool.tensor_scalar(small[:], ez[:], -0.5, 1.0, ALU.mult, ALU.add).then_inc(slope_ready, 1)
                after(pool, slope_ready, phase + 1)
                pool.tensor_tensor(small[:], small[:], ez[:], ALU.mult).then_inc(small_ready, 1)

            def softplus(phase):
                after(pool, log1p_ready, phase + 1)
                pool.tensor_tensor(delta[:], delta[:], pos[:], ALU.add).then_inc(delta_ready, 1)

            def times_C(b, s):
                n = UNITS * b + s
                after(pool, h_ready, n + 1)
                if not LEAD - 1 <= s < NCG:
                    after(pool, summed, UNITS // QUADS * b + (s - NCG) // QUADS + 1)
                if s % GROUPS == 0:
                    after(pool, C_ready, HALVES * (2 * b + s // GROUPS + 1))
                pool.tensor_tensor(ch[:, s % NCG, :], h[:, s % NH, :], C_rep[s // GROUPS][:], ALU.mult)\
                    .then_inc(ch_ready, 1)

            def units(i, first, last, now=True, following=True):
                for s in range(first, last):
                    if s == 16 and following:
                        after(pool, rstd_ready, i + 2)
                    if s in (19, UNITS + 3) and following:
                        phase = 2 * (i + 1) + s // UNITS
                        after(pool, e_ready, phase + 1)
                        after(pool, log1p_ready, phase)
                    if (now and s <= UNITS) or (following and s > UNITS):
                        times_C(*((i, s - 1) if s <= UNITS else (i + 1, s - 1 - UNITS)))
                    if s == 16 and following:
                        normalise()
                    if s == 19 and following:
                        small_log1p(2 * (i + 1))
                    if s == 21 and following:
                        softplus(2 * (i + 1))
                    if s == UNITS + 3 and following:
                        small_log1p(2 * (i + 1) + 1)
                    if s == 5 and now:
                        softplus(2 * i + 1)

            units(-1, 12, UNITS + LEAD, now=False)
            with pool.Fori(0, NB - 1) as i:
                units(i, LEAD, UNITS + LEAD)
            units(NB - 1, LEAD, UNITS + 1, following=False)

        @block.scalar
        def _(act):
            act.wait_ge(small_loaded, 16 * 13)
            act.wait_ge(setup_taken[1], 1)
            act.activation(neg_A[:], a_in[:], ACT.Exp).then_inc(act_step, 1)
            act.wait_ge(act_step, 1)
            act.mul(neg_A[:], neg_A[:], -1.0).then_inc(act_step, 1)
            act.mul(s_net[:, 0:1], s_in[:, 0:1], 4.0).then_inc(act_step, 1)
            act.mul(s_net[:, 1:2], s_in[:, 1:2], 2.0).then_inc(act_step, 1)
            act.mul(s_net[:, 2:3], s_in[:, 2:3], 1.0).then_inc(act_step, 1)
            act.wait_ge(act_step, 5)
            act.wait_ge(spread_built, 1)
            act.copy(spread[:].rearrange("p g m -> p (g m)"), a[:, 0, :]).then_inc(const_ready, 1)
            act.wait_ge(const_ready, 1)

            def decay(b, s):
                n = UNITS * b + s
                k = s % GROUPS
                after(act, d_rep_ready, n + 1)
                after(act, h_ready, n - 1)
                act.activation(a[:, s % 2, :], d_rep[:], ACT.Exp,
                               scale=neg_A[:, s // GROUPS, group(k):group(k) + 1]).then_inc(a_ready, 1)

            def evacuate(b, step, arg, half, bank, use):
                after(act, work_full[bank], use + 1)
                src = work[bank]
                if step == "turn":
                    after(act, u_ready, 2 * b)
                    act.copy(xnT[:, cols(half)], src[:]).then_inc(xnT_ready, 1)
                elif step == "delta":
                    phase = 2 * b + arg
                    after(act, hi_ready[1], phase)
                    after(act, lo_ready[1], phase)
                    after(act, small_ready, phase)
                    act.activation(ez[:, cols(half)], src[:], ACT.Abs, bias=bias_dt[:, arg:arg + 1])
                    act.activation(pos[:, cols(half)], src[:], ACT.Relu, bias=bias_dt[:, arg:arg + 1])\
                        .then_inc(z_taken, 1)
                elif step == "B":
                    act.copy(B_rep[arg][:, cols(half)], src[:]).then_inc(B_ready, 1)
                elif step == "C":
                    act.copy(C_rep[arg][:, cols(half)], src[:]).then_inc(C_ready, 1)
                elif step == "net0":
                    act.activation(h1[:, arg, :], src[:], ACT.Relu, scale=s_net[:, 0:1]).then_inc(h1_ready, 1)
                elif step == "net1":
                    act.activation(h2[:, arg, :], src[:], ACT.Relu, scale=s_net[:, 1:2]).then_inc(h2_ready, 1)
                elif step == "net2":
                    act.activation(gate[:, cols(half)], src[:], ACT.Silu, scale=s_net[:, 2:3])\
                        .then_inc(gate_ready, 1)

            def log_of(phase):
                after(act, z_taken, HALVES * (phase + 1))
                act.activation(ez[:], ez[:], ACT.Exp, scale=-1.0).then_inc(e_ready, 1)
                after(act, e_ready, phase + 1)
                after(act, lo_ready[0], phase)
                after(act, u_ready, phase)
                act.activation(delta[:], ez[:], ACT.Ln, bias=1.0).then_inc(ln_ready, 1)

            def high(n, phase):
                after(act, delta_ready if n == 0 else u_ready, phase + 1)
                after(act, stacked[n], 64 * phase)
                act.copy(hi[n][:], (delta if n == 0 else pos)[:]).then_inc(hi_ready[n], 1)

            def units(i, sec, first, last, now=True, following=True):
                for s in range(first, last):
                    b, u = (i, s) if s < UNITS else (i + 1, s - UNITS)
                    if (now and s < UNITS) or (following and s >= UNITS):
                        decay(b, u)
                    for b, step, arg, half, bank, use, _ in sec.at(s, i):
                        if step != "store":
                            evacuate(b, step, arg, half, bank, use)
                    if s == 14 and following:
                        after(act, moments_ready, i + 2)
                        act.activation(std[:], moments[:, :, 1], ACT.Sqrt, bias=eps[:, 0:1]).then_inc(std_ready, 1)
                    if s == 18 and following:
                        log_of(2 * (i + 1))
                    if s == 22 and following:
                        high(0, 2 * (i + 1))
                    if s == 23 and following:
                        high(1, 2 * (i + 1))
                    if s == UNITS + 2 and following:
                        log_of(2 * (i + 1) + 1)
                    if s == 6 and now:
                        high(0, 2 * i + 1)
                    if s == 7 and now:
                        high(1, 2 * i + 1)

            units(-1, opening, 12, UNITS + LEAD, now=False)
            with act.Fori(0, NB - 1) as i:
                units(i, looped, LEAD, UNITS + LEAD)
            units(NB - 1, closing, LEAD, UNITS, following=False)

        @block.vector
        def _(dve):
            dve.memset(eps[:], EPS).then_inc(dve_step, 1)
            dve.wait_ge(small_loaded, 16 * 13)
            dve.wait_ge(nets_loaded, 16 * 3)
            dve.tensor_tensor(w0[:], k0_sb[:, 0, :], k0_sb[:, 1, :], ALU.subtract).then_inc(dve_step, 1)
            dve.tensor_scalar(w1[:], k1_sb[:], 2.0, -1.0, ALU.mult, ALU.add).then_inc(dve_step, 1)
            dve.tensor_scalar(w2[:], k2_sb[:], 2.0, -1.0, ALU.mult, ALU.add).then_inc(dve_step, 1)
            dve.tensor_tensor(skips[:, 2:3], skips[:, 0:1], skips[:, 1:2], ALU.add).then_inc(dve_step, 1)
            dve.wait_ge(ident_ready, 1)
            dve.wait_ge(dve_step, 5)
            dve.tensor_scalar(skip_diag[:], ident[:], skips[:, 2:3], None, ALU.mult).then_inc(dve_step, 1)
            dve.wait_ge(work_full[0], 1)
            for d in range(2):
                for w, at in ((w_B, R), (w_C, R + S)):
                    src = work[0][:, d * (R + 2 * S) + at:d * (R + 2 * S) + at + S]
                    for c in range(CH):
                        last = dve.tensor_copy(w[:, d, c * S:(c + 1) * S], src)
            last.then_inc(setup_taken[0], 1)
            dve.wait_ge(work_full[1], 1)
            dve.tensor_copy(a_in[:].rearrange("p d g -> p (d g)"), work[1][:, 2 * D:2 * D + 2 * GROUPS])
            dve.tensor_copy(dtT[:].rearrange("r d m -> r (d m)"), work[1][0:R, 0:2 * D]).then_inc(setup_taken[1], 1)
            dve.wait_ge(work_full[0], 2)
            dve.tensor_copy(w_delta[:].rearrange("r d m -> r (d m)"), work[0][:, 0:2 * D]).then_inc(setup_taken[0], 1)

            def statistics(b):
                after(dve, x_loaded, 16 * (b + 1))
                for j in range(TILES):
                    last = dve.bn_stats(stats[:, j, :], x_in[:, j, :])
                last.then_inc(stats_ready, 1)

            def aggregate():
                for j in range(TILES):
                    last = dve.bn_aggr(moments[:, j, :], stats[:, j, :])
                last.then_inc(moments_ready, 1)

            def inverse(b):
                after(dve, std_ready, b + 1)
                dve.reciprocal(rstd[:], std[:]).then_inc(rstd_ready, 1)

            def log1p(phase):
                after(dve, ln_ready, phase + 1)
                after(dve, small_ready, phase + 1)
                dve.scalar_tensor_tensor(out=delta[:], in0=delta[:], scalar=-LOG_SLACK, in1=small[:],
                                         op0=ALU.add, op1=ALU.max).then_inc(log1p_ready, 1)

            def delta_times_x(b, phase):
                after(dve, delta_ready, phase + 1)
                after(dve, xnT_ready, HALVES * (b + 1))
                dve.tensor_tensor(pos[:], delta[:], xnT[:], ALU.mult).then_inc(u_ready, 1)

            def low(n, phase):
                after(dve, hi_ready[n], phase + 1)
                dve.tensor_tensor(lo[n][:], (delta if n == 0 else pos)[:], hi[n][:].bitcast(F32), ALU.subtract)\
                    .then_inc(lo_ready[n], 1)

            def input_term(b, s):
                n = UNITS * b + s
                after(dve, u_rep_ready, n + 1)
                if s % GROUPS == 0:
                    after(dve, B_ready, HALVES * (2 * b + s // GROUPS + 1))
                after(dve, ch_ready, n - NH + 1)
                dve.tensor_tensor(h[:, s % NH, :], u_rep[:], B_rep[s // GROUPS][:], ALU.mult).then_inc(bx_ready, 1)

            def scan(b, s):
                n = UNITS * b + s
                after(dve, bx_ready, n + 1)
                after(dve, a_ready, n + 1)
                t = slice(None) if s < GROUPS else slice(None, None, -1)
                dve.tensor_tensor_scan(h[:, s % NH, t], a[:, s % 2, t], h[:, s % NH, t], 0.0, ALU.mult, ALU.add)\
                    .then_inc(h_ready, 1)

            def gate_y(b):
                after(dve, summed, UNITS // QUADS * (b + 1))
                after(dve, gate_ready, HALVES * (b + 1))
                dve.tensor_tensor(gated[:], y[:], gate[:], ALU.mult).then_inc(gated_ready, 1)

            def add_residual(b, half, bank, use):
                after(dve, work_full[bank], use + 1)
                after(dve, moved, 16 * (1 + HALVES) * b + 16)
                dve.tensor_tensor(x_out[:, half * TH:(half + 1) * TH, :],
                                  work[bank][:].rearrange("p (j d) -> p j d", d=D),
                                  x_res[:, half * TH:(half + 1) * TH, :], ALU.add).then_inc(out_ready, 1)

            def units(i, sec, first, last, now=True, following=True):
                for s in range(first, last):
                    if s == 13 and following:
                        after(dve, stats_ready, i + 2)
                        after(dve, xn_ready, i + 1)
                    if (now and s < UNITS) or (following and s >= UNITS):
                        input_term(*((i, s) if s < UNITS else (i + 1, s - UNITS)))
                    if (now and s <= UNITS) or (following and s > UNITS):
                        scan(*((i, s - 1) if s <= UNITS else (i + 1, s - 1 - UNITS)))
                    if s == 12 and following:
                        statistics(i + 1)
                    if s == 13 and following:
                        aggregate()
                    if s == 15 and following:
                        inverse(i + 1)
                    if s == 20 and following:
                        log1p(2 * (i + 1))
                    if s == 22 and following:
                        delta_times_x(i + 1, 2 * (i + 1))
                    if s == 23 and following:
                        low(0, 2 * (i + 1))
                    if s == 24 and following:
                        low(1, 2 * (i + 1))
                    if s == UNITS + 4 and following:
                        log1p(2 * (i + 1) + 1)
                    if s == 6 and now:
                        delta_times_x(i, 2 * i + 1)
                    if s == 7 and now:
                        low(0, 2 * i + 1)
                    if s == 8 and now:
                        low(1, 2 * i + 1)
                    if s == UNITS + 3 and now:
                        gate_y(i)
                    for b, step, arg, half, bank, use, _ in sec.at(s, i):
                        if step == "store":
                            add_residual(b, half, bank, use)

            units(-1, opening, 12, UNITS + LEAD, now=False)
            with dve.Fori(0, NB - 1) as i:
                units(i, looped, LEAD, UNITS + LEAD)
            units(NB - 1, closing, LEAD, UNITS + LEAD, following=False)

        @block.tensor
        def _(pe):
            pe.wait_ge(small_loaded, 16 * 13)
            pe.wait_ge(ident_ready, 1)
            W = R + 2 * S
            for d in range(2):
                last = pe.transpose(work[0][:, d * W:(d + 1) * W], xp_sb[:, d, :], ident[0:W, 0:W])
            last.then_inc(work_full[0], 1)
            for d in range(2):
                last = pe.transpose(work[1][0:R, d * D:(d + 1) * D], dt_sb[:, d, :], ident[:])
            for d in range(2):
                last = pe.transpose(work[1][:, 2 * D + d * GROUPS:2 * D + (d + 1) * GROUPS], a_nat[:, d, :],
                                    ident[0:GROUPS, 0:GROUPS])
            last.then_inc(work_full[1], 1)
            pe.wait_ge(setup_taken[0], 1)
            pe.wait_ge(setup_taken[1], 1)
            for d in range(2):
                last = pe.matmul(work[0][:, d * D:(d + 1) * D], xp_sb[0:R, d, :], dtT[:, d, :],
                                 start=True, stop=True)
            last.then_inc(work_full[0], 1)
            pe.wait_ge(dve_step, 6)
            pe.wait_ge(const_ready, 1)
            pe.wait_ge(gather_ready, 1)

            def replicate(b, s):
                n = UNITS * b + s
                d, g = s // GROUPS, group(s % GROUPS)
                t, sel = g // (GROUPS // 2), spread[:, g % (GROUPS // 2), :]
                if s % GROUPS == 0:
                    after(pe, stacked[0], 64 * (2 * b + d + 1))
                after(pe, a_ready, n)
                for half in range(HALVES):
                    last = pe.matmul(d_rep[:, cols(half)], sel, stack[d][0][:, t, cols(half)],
                                     start=True, stop=True)
                last.then_inc(d_rep_ready, 1)
                if s % GROUPS == 0:
                    after(pe, stacked[1], 64 * (2 * b + d + 1))
                after(pe, bx_ready, n)
                for half in range(HALVES):
                    last = pe.matmul(u_rep[:, cols(half)], sel, stack[d][1][:, t, cols(half)],
                                     start=True, stop=True)
                last.then_inc(u_rep_ready, 1)

            def sum_states(b, s):
                n = UNITS * b + s
                after(pe, ch_ready, n + 1)
                for half in range(HALVES):
                    for q in range(QUADS):
                        last = pe.matmul(y[q * Q:(q + 1) * Q, cols(half)], gather[:, (s % GROUPS) // QUADS, :],
                                         ch[:, (s - QUADS + 1 + q) % NCG, cols(half)], start=False,
                                         stop=(s == UNITS - 1), skip_group_check=True)
                last.then_inc(summed, 1)

            def skip_term(b):
                after(pe, gated_ready, b)
                for half in range(HALVES):
                    pe.matmul(y[:, cols(half)], skip_diag[:], xnT[:, cols(half)], start=True, stop=False,
                              skip_group_check=True)

            def bank_free(sec, i, p):
                if p >= 2:
                    after(pe, *taken(i, *sec.steps[p - 2]))
                elif sec is opening:
                    after(pe, setup_taken[(SETUP + p) % 2], 1 + p)
                else:
                    after(pe, *taken(i - 1, *LATE[p - 2]))

            def background(b, step, arg, half, bank):
                dst = work[bank]
                if step == "turn":
                    if half == 0:
                        after(pe, xn_ready, b + 1)
                    for j in range(TH):
                        last = pe.transpose(dst[:, j * P:(j + 1) * P], x_in[:, half * TH + j, :], ident[:])
                elif step in ("delta", "B", "C"):
                    if step == "delta" and arg == 0 and half == 0:
                        after(pe, xnT_ready, HALVES * (b + 1))
                    w = {"delta": w_delta, "B": w_B, "C": w_C}[step]
                    last = pe.matmul(dst[:], w[:, arg, :], xnT[:, cols(half)], start=True, stop=True)
                elif step == "net0":
                    last = pe.matmul(dst[:], w0[:, arg * P:(arg + 1) * P], xnT[:, cols(half)],
                                     start=True, stop=True)
                elif step == "net1":
                    after(pe, h1_ready, FM * (HALVES * b + half + 1))
                    for t in range(FM):
                        last = pe.matmul(dst[:], w1[:, t, arg * P:(arg + 1) * P], h1[:, t, :],
                                         start=(t == 0), stop=(t == FM - 1))
                elif step == "net2":
                    after(pe, h2_ready, FM * (HALVES * b + half + 1))
                    for t in range(FM):
                        last = pe.matmul(dst[:], w2[:, t, :], h2[:, t, :], start=(t == 0), stop=(t == FM - 1))
                elif step == "store":
                    after(pe, gated_ready, b + 1)
                    for j in range(TH):
                        last = pe.transpose(dst[:, j * P:(j + 1) * P], gated[:, (half * TH + j) * P:(half * TH + j + 1) * P],
                                            ident[:])
                last.then_inc(work_full[bank], 1)

            def units(i, sec, first, last, now=True, following=True):
                for s in range(first, last):
                    if (now and s < UNITS) or (following and s >= UNITS):
                        replicate(*((i, s) if s < UNITS else (i + 1, s - UNITS)))
                    if s % QUADS == 2 and s >= 6 and now:
                        sum_states(i, s - 3)
                    if s == UNITS + 4 and following:
                        skip_term(i + 1)
                    for b, step, arg, half, bank, use, p in sec.at(s, i):
                        bank_free(sec, i, p)
                        background(b, step, arg, half, bank)

            units(-1, opening, 12, UNITS + LEAD, now=False)
            with pe.Fori(0, NB - 1) as i:
                units(i, looped, LEAD, UNITS + LEAD)
            units(NB - 1, closing, LEAD, UNITS + LEAD, following=False)


_PAIRS = ("x_proj", "dt_proj", "dt_bias", "A_log", "D_skip")


def kernel(**inputs):
    import numpy as np
    import concourse.bacc as bacc
    from concourse.bass_utils import run_bass_kernel_spmd

    a = {k: np.ascontiguousarray(v) for k, v in inputs.items()}
    arrays = {
        "x": a["L0_attn_x"],
        "x_proj0": a["L0_attn_x_proj_w"], "x_proj1": a["L0_attn_x_proj_b_w"],
        "dt_proj0": a["L0_attn_dt_proj_w"], "dt_proj1": a["L0_attn_dt_proj_b_w"],
        "dt_bias0": a["L0_attn_dt_proj_b"], "dt_bias1": a["L0_attn_dt_proj_b_b"],
        "A_log0": a["L0_attn_A_log"], "A_log1": a["L0_attn_A_b_log"],
        "D_skip0": a["L0_attn_D"], "D_skip1": a["L0_attn_D_b"],
        "k0": a["L0_ffn_k0"], "k1": a["L0_ffn_k1"],
        "k2": a["L0_ffn_k2"],
        "s0": a["L0_ffn_s0"].reshape(1, 1), "s1": a["L0_ffn_s1"].reshape(1, 1),
        "s2": a["L0_ffn_s2"].reshape(1, 1),
    }
    nc = bacc.Bacc("TRN2", target_bir_lowering=False, num_devices=1)
    ap = {n: nc.dram_tensor(f"in_{n}", v.shape, mybir.dt.from_np(v.dtype), kind="ExternalInput").ap()
          for n, v in arrays.items()}
    out = nc.dram_tensor("out", a["L0_attn_x"].shape, F32, kind="ExternalOutput").ap()
    pairs = [[ap[n + "0"], ap[n + "1"]] for n in _PAIRS]
    build_scan_and_gate(nc, ap["x"], *pairs, ap["k0"], ap["k1"], ap["k2"], [ap["s0"], ap["s1"], ap["s2"]], out)
    r = run_bass_kernel_spmd(nc, [{f"in_{n}": v for n, v in arrays.items()}], core_ids=[0])
    return r.results[0]["out"]
```

```python
from contextlib import ExitStack

import concourse.bass as bass
from concourse import mybir

F32 = mybir.dt.float32
F32R = mybir.dt.float32r
U8 = mybir.dt.uint8
ALU = mybir.AluOpType
ACT = mybir.ActivationFunctionType

P = 128
BANK = 512
EPS = 1e-5
EXP_AND_LN = "natural_log_exp_and_others"
LOG_SLACK = 7e-8


def after(eng, sem, count):
    if isinstance(count, int) and count <= 0:
        return
    eng.wait_ge(sem, count)


def build_scan_and_gate(nc, x, x_proj, dt_proj, dt_bias, A_log, D_skip, k0, k1, k2, scales, out):
    NB, L, D = x.shape
    S = A_log[0].shape[1]
    R = dt_proj[0].shape[1]
    F = k0.shape[1]
    CH = P // S
    GROUPS = D // CH
    UNITS = 2 * GROUPS
    HALVES = L // BANK
    TILES = L // P
    TH = TILES // HALVES
    FM = F // P
    QUADS = 4
    Q = P // QUADS
    PER_Q = GROUPS // QUADS
    NH = 4
    NCG = 8
    LEAD = 9
    assert D == P and F == BANK and HALVES == 2 and GROUPS == 16 and UNITS % NCG == 0

    def group(k):
        return PER_Q * (k % QUADS) + k // QUADS

    U = UNITS
    body = [
        (0, (9, 9, 9, 10), "net1", 2, 0), (0, (10, 10, 12, 12), "net1", 3, 0),
        (0, (12,), "net0", 0, 1), (0, (13,), "net0", 1, 1), (0, (13,), "net0", 2, 1), (0, (13,), "net0", 3, 1),
        (0, (14, 14, 16, 16), "net2", 0, 0), (1, (16,), "turn", 0, 0), (1, (16,), "turn", 0, 1),
        (0, (17, 17, 17, 18), "net1", 0, 1), (1, (18,), "delta", 0, 0), (1, (18,), "delta", 0, 1),
        (0, (20, 20, 20, 21), "net1", 1, 1), (0, (21, 21, 22, 22), "net1", 2, 1),
        (0, (24, 24, 24, 25), "net1", 3, 1), (1, (25,), "B", 0, 0), (1, (25,), "B", 0, 1),
        (1, (26,), "C", 0, 0), (1, (26,), "C", 0, 1), (0, (28, 28, 28, 29), "net2", 0, 1),
        (1, (29,), "net0", 0, 0), (1, (29,), "net0", 1, 0), (1, (30,), "net0", 2, 0), (1, (30,), "net0", 3, 0),
        (1, (U, U, U, U + 1), "net1", 0, 0), (1, (U + 1,), "delta", 1, 0), (1, (U + 1,), "delta", 1, 1),
        (1, (U + 2, U + 2, U + 4, U + 4), "net1", 1, 0), (1, (U + 4,), "B", 1, 0), (1, (U + 5,), "B", 1, 1),
        (0, (U + 6,), "store", 0, 0), (0, (U + 6,), "store", 0, 1),
        (1, (U + 8,), "C", 1, 0), (1, (U + 8,), "C", 1, 1)]
    start = [step for step in body if step[0] == 1]
    end = [step for step in body if step[0] == 0]
    SETUP = 3

    with ExitStack() as ctx:
        def sb(name, shape, dt=F32):
            return ctx.enter_context(nc.sbuf_tensor(name, shape, dt))

        def sem(name):
            return ctx.enter_context(nc.semaphore(name))

        ident = sb("ident", [P, P])
        spread = sb("spread", [P, GROUPS // 2, P], F32R)
        gather = sb("gather", [P, PER_Q, Q])
        skip_diag = sb("skip_diag", [P, P])
        w0 = sb("w0", [P, F])
        w1 = sb("w1", [P, FM, F])
        w2 = sb("w2", [P, FM, D])
        k0_sb = sb("k0_sb", [P, 2, F], U8)
        k1_sb = sb("k1_sb", [P, FM, F], U8)
        k2_sb = sb("k2_sb", [P, FM, D], U8)
        xp_sb = sb("xp_sb", [R + 2 * S, 2, D])
        dt_sb = sb("dt_sb", [D, 2, R])
        dtT = sb("dtT", [R, 2, D])
        w_delta = sb("w_delta", [D, 2, D])
        w_B = sb("w_B", [D, 2, P])
        w_C = sb("w_C", [D, 2, P])
        neg_A = sb("neg_A", [P, 2, GROUPS])
        a_nat = sb("a_nat", [GROUPS, 2, P])
        a_in = sb("a_in", [P, 2, GROUPS])
        bias_dt = sb("bias_dt", [D, 2])
        skips = sb("skips", [D, 3])
        s_in = sb("s_in", [P, 3])
        s_net = sb("s_net", [P, 3])
        eps = sb("eps", [P, 1])
        x_in = sb("x_in", [P, TILES, D])
        x_res = sb("x_res", [P, TILES, D])
        xnT = sb("xnT", [D, L])
        stats = sb("stats", [P, TILES, 6])
        moments = sb("moments", [P, TILES, 2])
        rough = sb("rough", [P, TILES])
        newton = sb("newton", [P, TILES])
        rstd = sb("rstd", [P, TILES])
        shift = sb("shift", [P, TILES])
        h1 = sb("h1", [P, FM, BANK])
        h2 = sb("h2", [P, FM, BANK])
        gate = sb("gate", [D, L])
        gated = sb("gated", [D, L])
        x_out = sb("x_out", [P, TILES, D])
        ez = sb("ez", [D, L])
        small = sb("small", [D, L])
        delta = sb("delta", [D, L])
        pos = sb("pos", [D, L])
        hi = [sb("delta_hi", [D, L], F32R), sb("u_hi", [D, L], F32R)]
        lo = [sb("delta_lo", [D, L], F32R), sb("u_lo", [D, L], F32R)]
        stack = [[sb(f"{n}_stack{d}", [P, 2, L], F32R) for n in ("delta", "u")] for d in range(2)]
        B_rep = [sb(f"B_rep{d}", [P, L]) for d in range(2)]
        C_rep = [sb(f"C_rep{d}", [P, L]) for d in range(2)]
        a = sb("a", [P, 2, L])
        h = sb("h", [P, NH, L])
        ch = sb("ch", [P, NCG, L])

        d_rep = ctx.enter_context(nc.psum_tensor("d_rep", [P, L], F32))
        u_rep = ctx.enter_context(nc.psum_tensor("u_rep", [P, L], F32))
        y = ctx.enter_context(nc.psum_tensor("y", [P, L], F32))
        work = [ctx.enter_context(nc.psum_tensor(f"work{n}", [P, BANK], F32)) for n in range(2)]

        small_loaded = sem("small_loaded")
        nets_loaded = sem("nets_loaded")
        x_loaded = sem("x_loaded")
        moved = sem("moved")
        ident_zero = sem("ident_zero")
        ident_ready = sem("ident_ready")
        spread_zero = sem("spread_zero")
        spread_built = sem("spread_built")
        gather_ones = sem("gather_ones")
        gather_cut = sem("gather_cut")
        gather_ready = sem("gather_ready")
        const_ready = sem("const_ready")
        dve_step = sem("dve_step")
        act_step = sem("act_step")
        work_full = [sem(f"work_full{n}") for n in range(2)]
        setup_taken = [sem(f"setup_taken{n}") for n in range(2)]
        moments_ready = sem("moments_ready")
        stats_ready = sem("stats_ready")
        log_var_ready = sem("log_var_ready")
        rough_ready = sem("rough_ready")
        newton_step = sem("newton_step")
        xn_ready = sem("xn_ready")
        xnT_ready = sem("xnT_ready")
        z_taken = sem("z_taken")
        e_ready = sem("e_ready")
        ln_ready = sem("ln_ready")
        slope_ready = sem("slope_ready")
        small_ready = sem("small_ready")
        log1p_ready = sem("log1p_ready")
        delta_ready = sem("delta_ready")
        u_ready = sem("u_ready")
        hi_ready = [sem("delta_hi_ready"), sem("u_hi_ready")]
        lo_ready = [sem("delta_lo_ready"), sem("u_lo_ready")]
        stacked = [sem("delta_stacked"), sem("u_stacked")]
        B_ready = sem("B_ready")
        C_ready = sem("C_ready")
        h1_ready = sem("h1_ready")
        h2_ready = sem("h2_ready")
        net_out = sem("net_out")
        gate_ready = sem("gate_ready")
        d_rep_ready = sem("d_rep_ready")
        a_ready = sem("a_ready")
        u_rep_ready = sem("u_rep_ready")
        bx_ready = sem("bx_ready")
        h_ready = sem("h_ready")
        ch_ready = sem("ch_ready")
        summed = sem("summed")
        gated_ready = sem("gated_ready")
        out_ready = sem("out_ready")

        def cols(half):
            return slice(half * BANK, (half + 1) * BANK)

        def taken(i, ahead, units, step, arg, half):
            b = i + ahead
            if step in ("net0", "net1"):
                return (h1_ready if step == "net0" else h2_ready), FM * (HALVES * b + half) + arg + 1
            if step in ("delta", "B", "C"):
                return {"delta": z_taken, "B": B_ready, "C": C_ready}[step], HALVES * (2 * b + arg) + half + 1
            return {"turn": xnT_ready, "net2": net_out, "store": out_ready}[step], HALVES * b + half + 1

        class Section:

            def __init__(self, steps, first, per_batch=0):
                self.steps, self.first, self.per_batch = steps, first, per_batch

            def parts(self, unit, i):
                for p, (ahead, units, step, arg, half) in enumerate(self.steps):
                    for t, u in enumerate(units):
                        if u == unit:
                            yield i + ahead, step, arg, half, (self.first + p) % 2, p, t

            def results(self, unit, i):
                for p, (ahead, units, step, arg, half) in enumerate(self.steps):
                    if units[-1] == unit:
                        n = self.first + p
                        yield i + ahead, step, arg, half, n % 2, n // 2 + i * (self.per_batch // 2)

        assert len(body) % 2 == 0
        opening = Section(start, SETUP)
        looped = Section(body, SETUP + len(start), len(body))
        closing = Section(end, SETUP + len(start) + (NB - 1) * len(body))

        block = ctx.enter_context(nc.Block())

        @block.sync
        def _(sp):
            def load_x(b):
                after(sp, xnT_ready, HALVES * b)
                sp.dma_start(x_in[:], x[b].rearrange("(j p) d -> p j d", p=P)).then_inc(x_loaded, 16)

            def load_residual(b):
                sp.dma_start(x_res[:], x[b].rearrange("(j p) d -> p j d", p=P)).then_inc(moved, 16)

            def stack_parts(b, d):
                for n in range(2):
                    after(sp, hi_ready[n], 2 * b + d + 1)
                    after(sp, lo_ready[n], 2 * b + d + 1)
                    for t in range(2):
                        rows = slice(t * P // 2, (t + 1) * P // 2)
                        sp.dma_start(stack[d][n][0:P // 2, t, :].bitcast(F32), hi[n][rows, :].bitcast(F32))\
                            .then_inc(stacked[n], 16)
                        sp.dma_start(stack[d][n][P // 2:P, t, :].bitcast(F32), lo[n][rows, :].bitcast(F32))\
                            .then_inc(stacked[n], 16)

            def store(b):
                for half in range(HALVES):
                    after(sp, out_ready, HALVES * b + half + 1)
                    sp.dma_start(out[b, half * BANK:(half + 1) * BANK, :].rearrange("(j p) d -> p j d", p=P),
                                 x_out[:, half * TH:(half + 1) * TH, :]).then_inc(moved, 16)

            load_x(0)
            for d in range(2):
                sp.dma_start(xp_sb[:, d, :], x_proj[d]).then_inc(small_loaded, 16)
                sp.dma_start(dt_sb[:, d, :], dt_proj[d]).then_inc(small_loaded, 16)
                sp.dma_start(bias_dt[:, d:d + 1], dt_bias[d].rearrange("(p a) -> p a", a=1)).then_inc(small_loaded, 16)
                sp.dma_start(skips[:, d:d + 1], D_skip[d].rearrange("(p a) -> p a", a=1)).then_inc(small_loaded, 16)
                sp.dma_start(a_nat[:, d, :], A_log[d].rearrange("(g c) s -> g (c s)", c=CH)).then_inc(small_loaded, 16)
            for n in range(3):
                sp.dma_start(s_in[:, n:n + 1], scales[n].partition_broadcast(P)).then_inc(small_loaded, 16)
            sp.dma_start(k0_sb[:], k0.rearrange("(t p) n -> p t n", p=P)).then_inc(nets_loaded, 16)
            sp.dma_start(k1_sb[:], k1.rearrange("(t p) n -> p t n", p=P)).then_inc(nets_loaded, 16)
            sp.dma_start(k2_sb[:], k2.rearrange("(t p) n -> p t n", p=P)).then_inc(nets_loaded, 16)
            stack_parts(0, 0)
            with sp.Fori(0, NB - 1) as i:
                load_x(i + 1)
                stack_parts(i, 1)
                load_residual(i)
                stack_parts(i + 1, 0)
                store(i)
            stack_parts(NB - 1, 1)
            load_residual(NB - 1)
            store(NB - 1)
            sp.wait_ge(moved, 16 * (1 + HALVES) * NB)

        @block.gpsimd
        def _(pool):
            pool.memset(ident[:], 0.0).then_inc(ident_zero, 1)
            pool.wait_ge(ident_zero, 1)
            pool.affine_select(out=ident[:], in_=ident[:], compare_op=ALU.not_equal, fill=1.0, base=0,
                               pattern=[[-1, P]], channel_multiplier=1).then_inc(ident_ready, 1)
            flat = a[:, 0, :]
            pool.memset(flat, 0.0).then_inc(spread_zero, 1)
            for n in range(2):
                pool.wait_ge(spread_zero, n + 1)
                pool.affine_select(out=flat.rearrange("p (g c s) -> p g c s", g=GROUPS // 2, s=S),
                                   in_=flat.rearrange("p (g c s) -> p g c s", g=GROUPS // 2, s=S),
                                   compare_op=ALU.not_equal, fill=1.0, base=-n * P // 2,
                                   pattern=[[-CH, GROUPS // 2], [-1, CH], [0, S]],
                                   channel_multiplier=1).then_inc(spread_built if n else spread_zero, 1)
            pool.memset(gather[:], 1.0).then_inc(gather_ones, 1)
            pool.wait_ge(gather_ones, 1)
            pool.affine_select(out=gather[:], in_=gather[:], compare_op=ALU.is_ge, fill=0.0, base=0,
                               pattern=[[S * CH, PER_Q], [-S, Q]], channel_multiplier=1).then_inc(gather_cut, 1)
            pool.wait_ge(gather_cut, 1)
            pool.affine_select(out=gather[:], in_=gather[:], compare_op=ALU.is_ge, fill=0.0, base=S - 1,
                               pattern=[[-S * CH, PER_Q], [S, Q]], channel_multiplier=-1).then_inc(gather_ready, 1)

            def small_log1p(phase):
                pool.tensor_scalar(small[:], ez[:], -0.5, 1.0, ALU.mult, ALU.add).then_inc(slope_ready, 1)
                after(pool, slope_ready, phase + 1)
                pool.tensor_tensor(small[:], small[:], ez[:], ALU.mult).then_inc(small_ready, 1)

            def softplus(phase):
                after(pool, log1p_ready, phase + 1)
                pool.tensor_tensor(delta[:], delta[:], pos[:], ALU.add).then_inc(delta_ready, 1)

            def times_C(b, s):
                n = UNITS * b + s
                after(pool, h_ready, n + 1)
                after(pool, summed, UNITS // QUADS * b + (s - NCG) // QUADS + 1)
                if s % GROUPS == 0:
                    after(pool, C_ready, HALVES * (2 * b + s // GROUPS + 1))
                pool.tensor_tensor(ch[:, s % NCG, :], h[:, s % NH, :], C_rep[s // GROUPS][:], ALU.mult)\
                    .then_inc(ch_ready, 1)

            def units(i, first, last, now=True, following=True):
                for s in range(first, last):
                    if s in (20, UNITS + 3) and following:
                        phase = 2 * (i + 1) + s // UNITS
                        after(pool, e_ready, phase + 1)
                        after(pool, log1p_ready, phase)
                    if (now and s <= UNITS) or (following and s > UNITS):
                        times_C(*((i, s - 1) if s <= UNITS else (i + 1, s - 1 - UNITS)))
                    if s == 20 and following:
                        small_log1p(2 * (i + 1))
                    if s == 23 and following:
                        softplus(2 * (i + 1))
                    if s == UNITS + 3 and following:
                        small_log1p(2 * (i + 1) + 1)
                    if s == UNITS + 6 and following:
                        softplus(2 * (i + 1) + 1)

            units(-1, LEAD, UNITS + LEAD, now=False)
            with pool.Fori(0, NB - 1) as i:
                units(i, LEAD, UNITS + LEAD)
            units(NB - 1, LEAD, UNITS + 1, following=False)

        @block.scalar
        def _(act):
            act.preload_act_table_set(EXP_AND_LN)
            act.wait_ge(small_loaded, 16 * 13)
            act.wait_ge(setup_taken[1], 1)
            act.activation(neg_A[:], a_in[:], ACT.Exp).then_inc(act_step, 1)
            act.wait_ge(act_step, 1)
            act.mul(neg_A[:], neg_A[:], -1.0).then_inc(act_step, 1)
            act.mul(s_net[:, 0:1], s_in[:, 0:1], 4.0).then_inc(act_step, 1)
            act.mul(s_net[:, 1:2], s_in[:, 1:2], 2.0).then_inc(act_step, 1)
            act.mul(s_net[:, 2:3], s_in[:, 2:3], 1.0).then_inc(act_step, 1)
            act.wait_ge(act_step, 5)
            act.wait_ge(spread_built, 1)
            act.copy(spread[:].rearrange("p g m -> p (g m)"), a[:, 0, :]).then_inc(const_ready, 1)
            act.wait_ge(const_ready, 1)

            def decay(b, s):
                n = UNITS * b + s
                k = s % GROUPS
                after(act, d_rep_ready, n + 1)
                after(act, h_ready, n - 1)
                act.activation(a[:, s % 2, :], d_rep[:], ACT.Exp,
                               scale=neg_A[:, s // GROUPS, group(k):group(k) + 1]).then_inc(a_ready, 1)

            def evacuate(b, step, arg, half, bank, use):
                after(act, work_full[bank], use + 1)
                src = work[bank]
                if step == "turn":
                    after(act, u_ready, 2 * b)
                    act.copy(xnT[:, cols(half)], src[:]).then_inc(xnT_ready, 1)
                elif step == "delta":
                    phase = 2 * b + arg
                    after(act, hi_ready[1], phase)
                    after(act, lo_ready[1], phase)
                    after(act, small_ready, phase)
                    act.activation(ez[:, cols(half)], src[:], ACT.Abs, bias=bias_dt[:, arg:arg + 1])
                    act.activation(pos[:, cols(half)], src[:], ACT.Relu, bias=bias_dt[:, arg:arg + 1])\
                        .then_inc(z_taken, 1)
                elif step == "B":
                    act.copy(B_rep[arg][:, cols(half)], src[:]).then_inc(B_ready, 1)
                elif step == "C":
                    act.copy(C_rep[arg][:, cols(half)], src[:]).then_inc(C_ready, 1)
                elif step == "net0":
                    act.activation(h1[:, arg, :], src[:], ACT.Relu, scale=s_net[:, 0:1]).then_inc(h1_ready, 1)
                elif step == "net1":
                    act.activation(h2[:, arg, :], src[:], ACT.Relu, scale=s_net[:, 1:2]).then_inc(h2_ready, 1)
                elif step == "net2":
                    if half == 0:
                        act.copy(gate[:, cols(0)], src[:]).then_inc(net_out, 1)
                    else:
                        act.activation(gate[:, cols(1)], src[:], ACT.Silu, scale=s_net[:, 2:3]).then_inc(net_out, 1)
                        after(act, net_out, HALVES * b + 1)
                        act.activation(gate[:, cols(0)], gate[:, cols(0)], ACT.Silu, scale=s_net[:, 2:3])\
                            .then_inc(gate_ready, 1)
                        act.preload_act_table_set(EXP_AND_LN)

            def rough_rstd(b):
                after(act, moments_ready, b + 1)
                act.activation(rough[:], moments[:, :, 1], ACT.Ln, bias=eps[:, 0:1]).then_inc(log_var_ready, 1)
                after(act, log_var_ready, b + 1)
                act.activation(rough[:], rough[:], ACT.Exp, scale=-0.5).then_inc(rough_ready, 1)

            def normalise(b):
                after(act, newton_step, 4 * (b + 1))
                for j in range(TILES):
                    last = act.activation(x_in[:, j, :], x_in[:, j, :], ACT.Identity, scale=rstd[:, j:j + 1],
                                          bias=shift[:, j:j + 1])
                last.then_inc(xn_ready, 1)

            def log_of(phase):
                after(act, z_taken, HALVES * (phase + 1))
                act.activation(ez[:], ez[:], ACT.Exp, scale=-1.0).then_inc(e_ready, 1)
                after(act, e_ready, phase + 1)
                after(act, lo_ready[0], phase)
                after(act, u_ready, phase)
                act.activation(delta[:], ez[:], ACT.Ln, bias=1.0).then_inc(ln_ready, 1)

            def high(n, phase):
                after(act, delta_ready if n == 0 else u_ready, phase + 1)
                after(act, stacked[n], 64 * phase)
                act.copy(hi[n][:], (delta if n == 0 else pos)[:]).then_inc(hi_ready[n], 1)

            def units(i, sec, first, last, now=True, following=True):
                for s in range(first, last):
                    b, u = (i, s) if s < UNITS else (i + 1, s - UNITS)
                    if (now and s < UNITS) or (following and s >= UNITS):
                        decay(b, u)
                    for b, step, arg, half, bank, use in sec.results(s, i):
                        if step != "store":
                            evacuate(b, step, arg, half, bank, use)
                    if s == 11 and following:
                        rough_rstd(i + 1)
                    if s == 13 and following:
                        normalise(i + 1)
                    if s == 19 and following:
                        log_of(2 * (i + 1))
                    if s == 25 and following:
                        high(0, 2 * (i + 1))
                    if s == 26 and following:
                        high(1, 2 * (i + 1))
                    if s == UNITS + 2 and following:
                        log_of(2 * (i + 1) + 1)
                    if s == 10 and now:
                        high(0, 2 * i + 1)
                    if s == 11 and now:
                        high(1, 2 * i + 1)

            units(-1, opening, LEAD, UNITS + LEAD, now=False)
            with act.Fori(0, NB - 1) as i:
                units(i, looped, LEAD, UNITS + LEAD)
            units(NB - 1, closing, LEAD, UNITS, following=False)

        @block.vector
        def _(dve):
            dve.memset(eps[:], EPS).then_inc(dve_step, 1)
            dve.wait_ge(small_loaded, 16 * 13)
            dve.wait_ge(nets_loaded, 16 * 3)
            dve.tensor_tensor(w0[:], k0_sb[:, 0, :], k0_sb[:, 1, :], ALU.subtract).then_inc(dve_step, 1)
            dve.tensor_scalar(w1[:], k1_sb[:], 2.0, -1.0, ALU.mult, ALU.add).then_inc(dve_step, 1)
            dve.tensor_scalar(w2[:], k2_sb[:], 2.0, -1.0, ALU.mult, ALU.add).then_inc(dve_step, 1)
            dve.tensor_tensor(skips[:, 2:3], skips[:, 0:1], skips[:, 1:2], ALU.add).then_inc(dve_step, 1)
            dve.wait_ge(ident_ready, 1)
            dve.wait_ge(dve_step, 5)
            dve.tensor_scalar(skip_diag[:], ident[:], skips[:, 2:3], None, ALU.mult).then_inc(dve_step, 1)
            dve.wait_ge(work_full[0], 1)
            for d in range(2):
                for w, at in ((w_B, R), (w_C, R + S)):
                    src = work[0][:, d * (R + 2 * S) + at:d * (R + 2 * S) + at + S]
                    last = dve.tensor_copy(w[:, d, :].rearrange("p (c s) -> p c s", s=S),
                                           src.unsqueeze(1).to_broadcast([D, CH, S]))
            last.then_inc(setup_taken[0], 1)
            dve.wait_ge(work_full[1], 1)
            dve.tensor_copy(a_in[:].rearrange("p d g -> p (d g)"), work[1][:, 2 * D:2 * D + 2 * GROUPS])
            dve.tensor_copy(dtT[:].rearrange("r d m -> r (d m)"), work[1][0:R, 0:2 * D]).then_inc(setup_taken[1], 1)
            dve.wait_ge(work_full[0], 2)
            dve.tensor_copy(w_delta[:].rearrange("r d m -> r (d m)"), work[0][:, 0:2 * D]).then_inc(setup_taken[0], 1)

            def statistics(b):
                after(dve, x_loaded, 16 * (b + 1))
                for j in range(TILES):
                    last = dve.bn_stats(stats[:, j, :], x_in[:, j, :])
                last.then_inc(stats_ready, 1)

            def aggregate():
                for j in range(TILES):
                    last = dve.bn_aggr(moments[:, j, :], stats[:, j, :])
                last.then_inc(moments_ready, 1)

            def inverse(b):
                after(dve, rough_ready, b + 1)
                dve.scalar_tensor_tensor(out=newton[:], in0=moments[:, :, 1], scalar=EPS, in1=rough[:],
                                         op0=ALU.add, op1=ALU.mult).then_inc(newton_step, 1)
                after(dve, newton_step, 4 * b + 1)
                dve.scalar_tensor_tensor(out=newton[:], in0=newton[:], scalar=-0.5, in1=rough[:],
                                         op0=ALU.mult, op1=ALU.mult).then_inc(newton_step, 1)
                after(dve, newton_step, 4 * b + 2)
                dve.scalar_tensor_tensor(out=rstd[:], in0=newton[:], scalar=1.5, in1=rough[:],
                                         op0=ALU.add, op1=ALU.mult).then_inc(newton_step, 1)
                after(dve, newton_step, 4 * b + 3)
                dve.scalar_tensor_tensor(out=shift[:], in0=moments[:, :, 0], scalar=-1.0, in1=rstd[:],
                                         op0=ALU.mult, op1=ALU.mult).then_inc(newton_step, 1)

            def log1p(phase):
                after(dve, ln_ready, phase + 1)
                after(dve, small_ready, phase + 1)
                dve.scalar_tensor_tensor(out=delta[:], in0=delta[:], scalar=-LOG_SLACK, in1=small[:],
                                         op0=ALU.add, op1=ALU.max).then_inc(log1p_ready, 1)

            def delta_times_x(b, phase):
                after(dve, delta_ready, phase + 1)
                after(dve, xnT_ready, HALVES * (b + 1))
                dve.tensor_tensor(pos[:], delta[:], xnT[:], ALU.mult).then_inc(u_ready, 1)

            def low(n, phase):
                after(dve, hi_ready[n], phase + 1)
                dve.tensor_tensor(lo[n][:], (delta if n == 0 else pos)[:], hi[n][:].bitcast(F32), ALU.subtract)\
                    .then_inc(lo_ready[n], 1)

            def input_term(b, s):
                n = UNITS * b + s
                after(dve, u_rep_ready, n + 1)
                if s % GROUPS == 0:
                    after(dve, B_ready, HALVES * (2 * b + s // GROUPS + 1))
                after(dve, ch_ready, n - NH + 1)
                dve.tensor_tensor(h[:, s % NH, :], u_rep[:], B_rep[s // GROUPS][:], ALU.mult).then_inc(bx_ready, 1)

            def scan(b, s):
                n = UNITS * b + s
                after(dve, bx_ready, n + 1)
                after(dve, a_ready, n + 1)
                t = slice(None) if s < GROUPS else slice(None, None, -1)
                dve.tensor_tensor_scan(h[:, s % NH, t], a[:, s % 2, t], h[:, s % NH, t], 0.0, ALU.mult, ALU.add)\
                    .then_inc(h_ready, 1)

            def gate_y(b):
                after(dve, summed, UNITS // QUADS * (b + 1))
                after(dve, gate_ready, b + 1)
                dve.tensor_tensor(gated[:], y[:], gate[:], ALU.mult).then_inc(gated_ready, 1)

            def add_residual(b, half, bank, use):
                after(dve, work_full[bank], use + 1)
                after(dve, moved, 16 * (1 + HALVES) * b + 16)
                dve.tensor_tensor(x_out[:, half * TH:(half + 1) * TH, :],
                                  work[bank][:].rearrange("p (j d) -> p j d", d=D),
                                  x_res[:, half * TH:(half + 1) * TH, :], ALU.add).then_inc(out_ready, 1)

            def units(i, sec, first, last, now=True, following=True):
                for s in range(first, last):
                    if s == 10 and following:
                        after(dve, stats_ready, i + 2)
                        after(dve, xn_ready, i + 1)
                    if (now and s < UNITS) or (following and s >= UNITS):
                        input_term(*((i, s) if s < UNITS else (i + 1, s - UNITS)))
                    if (now and s <= UNITS) or (following and s > UNITS):
                        scan(*((i, s - 1) if s <= UNITS else (i + 1, s - 1 - UNITS)))
                    if s == 9 and following:
                        statistics(i + 1)
                    if s == 10 and following:
                        aggregate()
                    if s == 12 and following:
                        inverse(i + 1)
                    if s == 22 and following:
                        log1p(2 * (i + 1))
                    if s == 25 and following:
                        delta_times_x(i + 1, 2 * (i + 1))
                    if s == 26 and following:
                        low(0, 2 * (i + 1))
                    if s == 27 and following:
                        low(1, 2 * (i + 1))
                    if s == UNITS + 5 and following:
                        log1p(2 * (i + 1) + 1)
                    if s == 10 and now:
                        delta_times_x(i, 2 * i + 1)
                    if s == 11 and now:
                        low(0, 2 * i + 1)
                    if s == 12 and now:
                        low(1, 2 * i + 1)
                    if s == UNITS + 4 and now:
                        gate_y(i)
                    for b, step, arg, half, bank, use in sec.results(s, i):
                        if step == "store":
                            add_residual(b, half, bank, use)

            units(-1, opening, LEAD, UNITS + LEAD, now=False)
            with dve.Fori(0, NB - 1) as i:
                units(i, looped, LEAD, UNITS + LEAD)
            units(NB - 1, closing, LEAD, UNITS + LEAD, following=False)

        @block.tensor
        def _(pe):
            pe.wait_ge(small_loaded, 16 * 13)
            pe.wait_ge(ident_ready, 1)
            W = R + 2 * S
            for d in range(2):
                last = pe.transpose(work[0][:, d * W:(d + 1) * W], xp_sb[:, d, :], ident[0:W, 0:W])
            last.then_inc(work_full[0], 1)
            for d in range(2):
                last = pe.transpose(work[1][0:R, d * D:(d + 1) * D], dt_sb[:, d, :], ident[:])
            for d in range(2):
                last = pe.transpose(work[1][:, 2 * D + d * GROUPS:2 * D + (d + 1) * GROUPS], a_nat[:, d, :],
                                    ident[0:GROUPS, 0:GROUPS])
            last.then_inc(work_full[1], 1)
            pe.wait_ge(setup_taken[0], 1)
            pe.wait_ge(setup_taken[1], 1)
            for d in range(2):
                last = pe.matmul(work[0][:, d * D:(d + 1) * D], xp_sb[0:R, d, :], dtT[:, d, :],
                                 start=True, stop=True)
            last.then_inc(work_full[0], 1)
            pe.wait_ge(dve_step, 6)
            pe.wait_ge(const_ready, 1)
            pe.wait_ge(gather_ready, 1)

            def selected(s):
                d, g = s // GROUPS, group(s % GROUPS)
                return d, g // (GROUPS // 2), spread[:, g % (GROUPS // 2), :]

            def replicate_delta(b, s):
                n = UNITS * b + s
                d, t, sel = selected(s)
                if s % GROUPS == 0:
                    after(pe, stacked[0], 64 * (2 * b + d + 1))
                after(pe, a_ready, n)
                for half in range(HALVES):
                    last = pe.matmul(d_rep[:, cols(half)], sel, stack[d][0][:, t, cols(half)],
                                     start=True, stop=True)
                last.then_inc(d_rep_ready, 1)

            def replicate_u(b, s):
                n = UNITS * b + s
                d, t, sel = selected(s)
                if s % GROUPS == 0:
                    after(pe, stacked[1], 64 * (2 * b + d + 1))
                after(pe, bx_ready, n)
                for half in range(HALVES):
                    last = pe.matmul(u_rep[:, cols(half)], sel, stack[d][1][:, t, cols(half)],
                                     start=True, stop=True)
                last.then_inc(u_rep_ready, 1)

            def sum_states(b, s):
                n = UNITS * b + s
                after(pe, ch_ready, n + 1)
                for half in range(HALVES):
                    for q in range(QUADS):
                        last = pe.matmul(y[q * Q:(q + 1) * Q, cols(half)], gather[:, (s % GROUPS) // QUADS, :],
                                         ch[:, (s - QUADS + 1 + q) % NCG, cols(half)], start=False,
                                         stop=(s == UNITS - 1), skip_group_check=True)
                last.then_inc(summed, 1)

            def skip_term(b):
                after(pe, gated_ready, b)
                for half in range(HALVES):
                    pe.matmul(y[:, cols(half)], skip_diag[:], xnT[:, cols(half)], start=True, stop=False,
                              skip_group_check=True)

            def bank_free(sec, i, p):
                if p >= 2:
                    after(pe, *taken(i, *sec.steps[p - 2]))
                elif sec is opening:
                    after(pe, setup_taken[(SETUP + p) % 2], 1 + p)
                else:
                    after(pe, *taken(i - 1, *body[p - 2]))

            def background(b, step, arg, half, bank, t):
                dst = work[bank]
                if step == "turn":
                    if half == 0:
                        after(pe, xn_ready, b + 1)
                    for j in range(TH):
                        last = pe.transpose(dst[:, j * P:(j + 1) * P], x_in[:, half * TH + j, :], ident[:])
                elif step in ("delta", "B", "C"):
                    if step == "delta" and arg == 0 and half == 0:
                        after(pe, xnT_ready, HALVES * (b + 1))
                    w = {"delta": w_delta, "B": w_B, "C": w_C}[step]
                    last = pe.matmul(dst[:], w[:, arg, :], xnT[:, cols(half)], start=True, stop=True)
                elif step == "net0":
                    last = pe.matmul(dst[:], w0[:, arg * P:(arg + 1) * P], xnT[:, cols(half)],
                                     start=True, stop=True)
                elif step == "net1":
                    if t == 0 and arg == 0:
                        after(pe, h1_ready, FM * (HALVES * b + half + 1))
                    last = pe.matmul(dst[:], w1[:, t, arg * P:(arg + 1) * P], h1[:, t, :],
                                     start=(t == 0), stop=(t == FM - 1))
                    if t < FM - 1:
                        return
                elif step == "net2":
                    if t == 0:
                        after(pe, h2_ready, FM * (HALVES * b + half + 1))
                    last = pe.matmul(dst[:], w2[:, t, :], h2[:, t, :], start=(t == 0), stop=(t == FM - 1))
                    if t < FM - 1:
                        return
                elif step == "store":
                    after(pe, gated_ready, b + 1)
                    for j in range(TH):
                        last = pe.transpose(dst[:, j * P:(j + 1) * P], gated[:, (half * TH + j) * P:(half * TH + j + 1) * P],
                                            ident[:])
                last.then_inc(work_full[bank], 1)

            def units(i, sec, first, last, now=True, following=True):
                for s in range(first, last):
                    if (now and s < UNITS) or (following and s >= UNITS):
                        replicate_u(*((i, s) if s < UNITS else (i + 1, s - UNITS)))
                    if s % QUADS == 3 and (now and s - 4 < UNITS or following and s - 4 >= UNITS):
                        sum_states(*((i, s - 4) if s - 4 < UNITS else (i + 1, s - 4 - UNITS)))
                    if s == UNITS + 6 and following:
                        skip_term(i + 1)
                    for b, step, arg, half, bank, p, t in sec.parts(s, i):
                        if t == 0:
                            bank_free(sec, i, p)
                        background(b, step, arg, half, bank, t)
                    if (now and s + 1 < UNITS) or (following and s + 1 >= UNITS):
                        replicate_delta(*((i, s + 1) if s + 1 < UNITS else (i + 1, s + 1 - UNITS)))

            units(-1, opening, LEAD, UNITS + LEAD, now=False)
            with pe.Fori(0, NB - 1) as i:
                units(i, looped, LEAD, UNITS + LEAD)
            units(NB - 1, closing, LEAD, UNITS + LEAD, following=False)


_PAIRS = ("x_proj", "dt_proj", "dt_bias", "A_log", "D_skip")


def kernel(**inputs):
    import numpy as np
    import concourse.bacc as bacc
    from concourse.bass_utils import run_bass_kernel_spmd

    a = {k: np.ascontiguousarray(v) for k, v in inputs.items()}
    arrays = {
        "x": a["L0_attn_x"],
        "x_proj0": a["L0_attn_x_proj_w"], "x_proj1": a["L0_attn_x_proj_b_w"],
        "dt_proj0": a["L0_attn_dt_proj_w"], "dt_proj1": a["L0_attn_dt_proj_b_w"],
        "dt_bias0": a["L0_attn_dt_proj_b"], "dt_bias1": a["L0_attn_dt_proj_b_b"],
        "A_log0": a["L0_attn_A_log"], "A_log1": a["L0_attn_A_b_log"],
        "D_skip0": a["L0_attn_D"], "D_skip1": a["L0_attn_D_b"],
        "k0": a["L0_ffn_k0"], "k1": a["L0_ffn_k1"],
        "k2": a["L0_ffn_k2"],
        "s0": a["L0_ffn_s0"].reshape(1, 1), "s1": a["L0_ffn_s1"].reshape(1, 1),
        "s2": a["L0_ffn_s2"].reshape(1, 1),
    }
    nc = bacc.Bacc("TRN2", target_bir_lowering=False, num_devices=1)
    ap = {n: nc.dram_tensor(f"in_{n}", v.shape, mybir.dt.from_np(v.dtype), kind="ExternalInput").ap()
          for n, v in arrays.items()}
    out = nc.dram_tensor("out", a["L0_attn_x"].shape, F32, kind="ExternalOutput").ap()
    pairs = [[ap[n + "0"], ap[n + "1"]] for n in _PAIRS]
    build_scan_and_gate(nc, ap["x"], *pairs, ap["k0"], ap["k1"], ap["k2"], [ap["s0"], ap["s1"], ap["s2"]], out)
    r = run_bass_kernel_spmd(nc, [{f"in_{n}": v for n, v in arrays.items()}], core_ids=[0])
    return r.results[0]["out"]
```

```python
from contextlib import ExitStack

import concourse.bass as bass
from concourse import mybir

F32 = mybir.dt.float32
F32R = mybir.dt.float32r
U8 = mybir.dt.uint8
ALU = mybir.AluOpType
ACT = mybir.ActivationFunctionType

P = 128
BANK = 512
EPS = 1e-5
EXP_AND_LN = "natural_log_exp_and_others"
LOG_SLACK = 7e-8


def after(eng, sem, count):
    if isinstance(count, int) and count <= 0:
        return
    eng.wait_ge(sem, count)


def build_scan_and_gate(nc, x, x_proj, dt_proj, dt_bias, A_log, D_skip, k0, k1, k2, scales, out):
    NB, L, D = x.shape
    S = A_log[0].shape[1]
    R = dt_proj[0].shape[1]
    F = k0.shape[1]
    CH = P // S
    GROUPS = D // CH
    UNITS = 2 * GROUPS
    HALVES = L // BANK
    TILES = L // P
    TH = TILES // HALVES
    FM = F // P
    QUADS = 4
    Q = P // QUADS
    PER_Q = GROUPS // QUADS
    NA = 3
    NH = 4
    NCG = 8
    LATE = (9, 31)
    GPSIMD_TILES = (3, 2)
    LEAD = 9
    assert D == P and F == BANK and HALVES == 2 and GROUPS == 16
    assert NB > 2 and UNITS % NCG == 0 and UNITS % NH == 0 and UNITS % NA == NA - 1

    def group(k):
        return PER_Q * (k % QUADS) + k // QUADS

    U = UNITS
    body = [
        (0, (9, 9, 9, 10), "net1", 2, 0), (0, (10, 10, 10, 10), "net1", 3, 0), (0, (11, 11, 12, 12), "net2", 0, 0),
        (0, (13,), "net0", 1, 1), (0, (14,), "net0", 0, 1), (0, (15,), "net0", 2, 1), (0, (16,), "net0", 3, 1),
        (1, (17,), "turn", 0, 0), (1, (17,), "turn", 0, 1), (1, (18,), "delta", 0, 0), (1, (18,), "delta", 0, 1),
        (1, (20,), "B", 0, 0), (1, (20,), "B", 0, 1), (0, (21, 21, 21, 21), "net1", 0, 1),
        (0, (22, 22, 22, 24), "net1", 1, 1), (0, (24, 24, 24, 24), "net1", 2, 1),
        (0, (25, 25, 25, 25), "net1", 3, 1), (1, (26,), "C", 0, 0), (1, (26,), "C", 0, 1),
        (0, (28, 28, 29, 29), "net2", 0, 1), (1, (29,), "net0", 0, 0), (1, (30,), "net0", 1, 0),
        (1, (31,), "net0", 2, 0), (1, (U + 1,), "net0", 3, 0), (1, (U + 2,), "delta", 1, 0),
        (1, (U + 2,), "delta", 1, 1), (1, (U + 3, U + 3, U + 3, U + 4), "net1", 0, 0), (1, (U + 4,), "B", 1, 0),
        (1, (U + 5,), "B", 1, 1), (1, (U + 5, U + 5, U + 5, U + 5), "net1", 1, 0), (0, (U + 6,), "store", 0, 0),
        (0, (U + 6,), "store", 0, 1), (1, (U + 8,), "C", 1, 0), (1, (U + 8,), "C", 1, 1)]
    AT = dict(
        u_1=9, high_delta_1=9, statistics=9, low_delta_1=10, high_u_1=10, low_u_1=11, aggregate=11, rough_rstd=12,
        inverse=13, normalise=14, low_h1_half1_gpsimd=15, low_h1_half1_vector=18, exp_0=19, small_0=20, log_0=22,
        log1p_0=23, softplus_0=23, high_delta_0=25, u_0=26, low_delta_0=27, high_u_0=28, low_u_0=28, silu=30,
        low_h1_half0_gpsimd=U, low_h1_half0_vector=U + 2, exp_1=U + 3, small_1=U + 3, log_1=U + 5, log1p_1=U + 6,
        softplus_1=U + 6, skip_term=U + 6, gate_y=U + 3)
    start = [(1, tuple(min(u, UNITS - 2) for u in units) if step == "net0" else units, step, arg, half)
             for ahead, units, step, arg, half in body if ahead == 1]
    end = [step for step in body if step[0] == 0]
    SETUP = 3
    FIRST_CONSTANTS = 27

    with ExitStack() as ctx:
        def sb(name, shape, dt=F32):
            return ctx.enter_context(nc.sbuf_tensor(name, shape, dt))

        def sem(name):
            return ctx.enter_context(nc.semaphore(name))

        ident = sb("ident", [P, P])
        spread = sb("spread", [P, GROUPS // 2, P], F32R)
        gather = sb("gather", [P, PER_Q, Q])
        skip_diag = sb("skip_diag", [P, P])
        w0 = sb("w0", [P, F])
        w1 = sb("w1", [P, FM, F], F32R)
        w2 = sb("w2", [P, FM, D])
        xp_sb = sb("xp_sb", [R + 2 * S, 2, D])
        dt_sb = sb("dt_sb", [D, 2, R])
        dtT = sb("dtT", [R, 2, D])
        w_delta = sb("w_delta", [D, 2, D])
        w_B = sb("w_B", [D, 2, P])
        w_C = sb("w_C", [D, 2, P])
        neg_A = sb("neg_A", [P, 2, GROUPS])
        a_nat = sb("a_nat", [GROUPS, 2, P])
        a_in = sb("a_in", [P, 2, GROUPS])
        bias_dt = sb("bias_dt", [D, 2])
        skips = sb("skips", [D, 3])
        s_in = sb("s_in", [P, 3])
        s_net = sb("s_net", [P, 3])
        eps = sb("eps", [P, 1])
        x_in = sb("x_in", [P, TILES, D])
        x_res = sb("x_res", [P, TILES, D])
        xnT = sb("xnT", [D, L])
        stats = sb("stats", [P, TILES, 6])
        moments = sb("moments", [P, TILES, 2])
        rough = sb("rough", [P, TILES])
        newton = sb("newton", [P, TILES])
        rstd = sb("rstd", [P, TILES])
        shift = sb("shift", [P, TILES])
        h1_lo = sb("h1_lo", [P, FM, BANK], F32R)
        h1_hi = sb("h1_hi", [P, FM, BANK], F32R)
        hidden = sb("hidden", [P, FM, BANK])
        gate = sb("gate", [D, L])
        ez = sb("ez", [D, L])
        small = sb("small", [D, L])
        delta = sb("delta", [D, L])
        pos = sb("pos", [D, L])
        hi = [sb("delta_hi", [D, L], F32R), sb("u_hi", [D, L], F32R)]
        lo = [sb("delta_lo", [D, L], F32R), sb("u_lo", [D, L], F32R)]
        stack = [[sb(f"{n}_stack{d}", [P, 2, L], F32R) for n in ("delta", "u")] for d in range(2)]
        B_rep = [sb(f"B_rep{d}", [P, L]) for d in range(2)]
        C_rep = [sb(f"C_rep{d}", [P, L]) for d in range(2)]
        a = sb("a", [P, NA, L])
        h = sb("h", [P, NH, L])
        ch = sb("ch", [P, NCG, L])
        k_in = ch[:, NCG - 1, :].bitcast(U8)
        k1_in = k_in[:, 0:FM * F].rearrange("p (t n) -> p t n", n=F)
        k0_in = k_in[:, FM * F:(FM + 2) * F].rearrange("p (t n) -> p t n", n=F)
        k2_in = k_in[:, (FM + 2) * F:(FM + 2) * F + FM * D].rearrange("p (t n) -> p t n", n=D)

        d_rep = ctx.enter_context(nc.psum_tensor("d_rep", [P, L], F32))
        u_rep = ctx.enter_context(nc.psum_tensor("u_rep", [P, L], F32))
        y = ctx.enter_context(nc.psum_tensor("y", [P, L], F32))
        work = [ctx.enter_context(nc.psum_tensor(f"work{n}", [P, BANK], F32)) for n in range(2)]

        proj_loaded = sem("proj_loaded")
        small_loaded = sem("small_loaded")
        nets_loaded = sem("nets_loaded")
        x_loaded = sem("x_loaded")
        moved = sem("moved")
        ident_zero = sem("ident_zero")
        ident_ready = sem("ident_ready")
        spread_zero = sem("spread_zero")
        spread_built = sem("spread_built")
        gather_ones = sem("gather_ones")
        gather_cut = sem("gather_cut")
        gather_ready = sem("gather_ready")
        const_ready = sem("const_ready")
        dve_step = sem("dve_step")
        act_step = sem("act_step")
        work_full = [sem(f"work_full{n}") for n in range(2)]
        setup_taken = [sem(f"setup_taken{n}") for n in range(2)]
        moments_ready = sem("moments_ready")
        stats_ready = sem("stats_ready")
        log_var_ready = sem("log_var_ready")
        rough_ready = sem("rough_ready")
        newton_step = sem("newton_step")
        xn_ready = sem("xn_ready")
        xnT_ready = sem("xnT_ready")
        z_taken = sem("z_taken")
        e_ready = sem("e_ready")
        ln_ready = sem("ln_ready")
        slope_ready = sem("slope_ready")
        small_ready = sem("small_ready")
        log1p_ready = sem("log1p_ready")
        delta_ready = sem("delta_ready")
        u_ready = sem("u_ready")
        hi_ready = [sem("delta_hi_ready"), sem("u_hi_ready")]
        lo_ready = [sem("delta_lo_ready"), sem("u_lo_ready")]
        stacked = [sem("delta_stacked"), sem("u_stacked")]
        B_ready = sem("B_ready")
        C_ready = sem("C_ready")
        h1_ready = sem("h1_ready")
        h1_lo_ready = [sem("h1_lo_ready_pool"), sem("h1_lo_ready_dve")]
        h2_ready = sem("h2_ready")
        net_out = sem("net_out")
        gate_ready = sem("gate_ready")
        d_rep_ready = sem("d_rep_ready")
        a_ready = sem("a_ready")
        u_rep_ready = sem("u_rep_ready")
        bx_ready = sem("bx_ready")
        h_ready = sem("h_ready")
        ch_ready = sem("ch_ready")
        summed = sem("summed")
        gated_ready = sem("gated_ready")
        out_ready = sem("out_ready")

        def cols(half):
            return slice(half * BANK, (half + 1) * BANK)

        def taken(i, ahead, units, step, arg, half):
            b = i + ahead
            if step in ("net0", "net1"):
                return (h1_ready if step == "net0" else h2_ready), FM * (HALVES * b + half) + arg + 1
            if step in ("delta", "B", "C"):
                return {"delta": z_taken, "B": B_ready, "C": C_ready}[step], HALVES * (2 * b + arg) + half + 1
            return {"turn": xnT_ready, "net2": net_out, "store": out_ready}[step], HALVES * b + half + 1

        class Section:

            def __init__(self, steps, first, per_batch=0):
                self.steps, self.first, self.per_batch = steps, first, per_batch

            def parts(self, unit, i):
                for p, (ahead, units, step, arg, half) in enumerate(self.steps):
                    for t, u in enumerate(units):
                        if u == unit:
                            yield i + ahead, step, arg, half, (self.first + p) % 2, p, t

            def results(self, unit, i):
                for p, (ahead, units, step, arg, half) in enumerate(self.steps):
                    if units[-1] == unit:
                        n = self.first + p
                        yield i + ahead, step, arg, half, n % 2, n // 2 + i * (self.per_batch // 2)

        assert len(body) % 2 == 0
        opening = Section(start, SETUP)
        looped = Section(body, SETUP + len(start), len(body))
        closing = Section(end, SETUP + len(start) + (NB - 1) * len(body))

        block = ctx.enter_context(nc.Block())

        @block.sync
        def _(sp):
            def load_x(b):
                after(sp, xnT_ready, HALVES * b)
                sp.dma_start(x_in[:], x[b].rearrange("(j p) d -> p j d", p=P)).then_inc(x_loaded, 16)

            def load_residual(b):
                after(sp, moved, 16 * (1 + HALVES) * b)
                sp.dma_start(x_res[:], x[b].rearrange("(j p) d -> p j d", p=P)).then_inc(moved, 16)

            def stack_parts(b, d):
                for n in range(2):
                    for place, part, ready in ((0, hi, hi_ready), (P // 2, lo, lo_ready)):
                        after(sp, ready[n], 2 * b + d + 1)
                        for t in range(2):
                            sp.dma_start(stack[d][n][place:place + P // 2, t, :].bitcast(F32),
                                         part[n][t * P // 2:(t + 1) * P // 2, :].bitcast(F32)).then_inc(stacked[n], 16)

            def store(b):
                for half in range(HALVES):
                    after(sp, out_ready, HALVES * b + half + 1)
                    sp.dma_start(out[b, half * BANK:(half + 1) * BANK, :].rearrange("(j p) d -> p j d", p=P),
                                 x_res[:, half * TH:(half + 1) * TH, :]).then_inc(moved, 16)

            load_x(0)
            for d in range(2):
                sp.dma_start(xp_sb[:, d, :], x_proj[d]).then_inc(proj_loaded, 16)
                sp.dma_start(dt_sb[:, d, :], dt_proj[d]).then_inc(proj_loaded, 16)
                sp.dma_start(a_nat[:, d, :], A_log[d].rearrange("(g c) s -> g (c s)", c=CH)).then_inc(proj_loaded, 16)
            for d in range(2):
                sp.dma_start(bias_dt[:, d:d + 1], dt_bias[d].rearrange("(p a) -> p a", a=1)).then_inc(small_loaded, 16)
                sp.dma_start(skips[:, d:d + 1], D_skip[d].rearrange("(p a) -> p a", a=1)).then_inc(small_loaded, 16)
            for n in range(3):
                sp.dma_start(s_in[:, n:n + 1], scales[n].partition_broadcast(P)).then_inc(small_loaded, 16)
            sp.dma_start(k0_in, k0.rearrange("(t p) n -> p t n", p=P)).then_inc(nets_loaded, 16)
            sp.dma_start(k1_in, k1.rearrange("(t p) n -> p t n", p=P)).then_inc(nets_loaded, 16)
            sp.dma_start(k2_in, k2.rearrange("(t p) n -> p t n", p=P)).then_inc(nets_loaded, 16)
            stack_parts(0, 0)
            load_x(1)
            load_residual(0)
            with sp.Fori(0, NB - 2) as i:
                stack_parts(i, 1)
                stack_parts(i + 1, 0)
                store(i)
                load_x(i + 2)
                load_residual(i + 1)
            stack_parts(NB - 2, 1)
            stack_parts(NB - 1, 0)
            store(NB - 2)
            load_residual(NB - 1)
            stack_parts(NB - 1, 1)
            store(NB - 1)
            sp.wait_ge(moved, 16 * (1 + HALVES) * NB)

        @block.gpsimd
        def _(pool):
            pool.memset(ident[:], 0.0).then_inc(ident_zero, 1)
            pool.wait_ge(ident_zero, 1)
            pool.affine_select(out=ident[:], in_=ident[:], compare_op=ALU.not_equal, fill=1.0, base=0,
                               pattern=[[-1, P]], channel_multiplier=1).then_inc(ident_ready, 1)
            flat = a[:, 0, :]
            pool.memset(flat, 0.0).then_inc(spread_zero, 1)
            for n in range(2):
                pool.wait_ge(spread_zero, n + 1)
                pool.affine_select(out=flat.rearrange("p (g c s) -> p g c s", g=GROUPS // 2, s=S),
                                   in_=flat.rearrange("p (g c s) -> p g c s", g=GROUPS // 2, s=S),
                                   compare_op=ALU.not_equal, fill=1.0, base=-n * P // 2,
                                   pattern=[[-CH, GROUPS // 2], [-1, CH], [0, S]],
                                   channel_multiplier=1).then_inc(spread_built if n else spread_zero, 1)
            pool.memset(gather[:], 1.0).then_inc(gather_ones, 1)
            pool.wait_ge(gather_ones, 1)
            pool.affine_select(out=gather[:], in_=gather[:], compare_op=ALU.is_ge, fill=0.0, base=0,
                               pattern=[[S * CH, PER_Q], [-S, Q]], channel_multiplier=1).then_inc(gather_cut, 1)
            pool.wait_ge(gather_cut, 1)
            pool.affine_select(out=gather[:], in_=gather[:], compare_op=ALU.is_ge, fill=0.0, base=S - 1,
                               pattern=[[-S * CH, PER_Q], [S, Q]], channel_multiplier=-1).then_inc(gather_ready, 1)

            def small_log1p(phase):
                after(pool, slope_ready, phase + 1)
                pool.tensor_tensor(small[:], small[:], ez[:], ALU.mult).then_inc(small_ready, 1)

            def low_h1(b, half):
                tiles = slice(0, GPSIMD_TILES[half])
                after(pool, h1_ready, FM * (HALVES * b + half) + GPSIMD_TILES[half])
                pool.tensor_tensor(h1_lo[:, tiles, :], hidden[:, tiles, :], h1_hi[:, tiles, :].bitcast(F32),
                                   ALU.subtract).then_inc(h1_lo_ready[0], 1)

            def softplus(phase):
                after(pool, log1p_ready, phase + 1)
                pool.tensor_tensor(delta[:], delta[:], pos[:], ALU.add).then_inc(delta_ready, 1)

            def times_C(b, s):
                n = UNITS * b + s
                after(pool, h_ready, n + 1)
                after(pool, summed, UNITS // QUADS * b + (s - NCG) // QUADS + 1)
                if s % GROUPS == 0:
                    after(pool, C_ready, HALVES * (2 * b + s // GROUPS + 1))
                pool.tensor_tensor(ch[:, s % NCG, :], h[:, s % NH, :], C_rep[s // GROUPS][:], ALU.mult)\
                    .then_inc(ch_ready, 1)

            def units(i, first, last, now=True, following=True):
                for s in range(first, last):
                    if (now and s <= UNITS) or (following and s > UNITS):
                        times_C(*((i, s - 1) if s <= UNITS else (i + 1, s - 1 - UNITS)))
                    if s == AT["small_0"] and following and now:
                        small_log1p(2 * (i + 1))
                    if s == AT["low_h1_half1_gpsimd"] and now:
                        low_h1(i, 1)
                    if s == AT["low_h1_half0_gpsimd"] and following:
                        low_h1(i + 1, 0)
                    if s == AT["softplus_0"] and following and now:
                        softplus(2 * (i + 1))
                    if s == AT["small_1"] and following:
                        small_log1p(2 * (i + 1) + 1)
                    if s == AT["softplus_1"] and following:
                        softplus(2 * (i + 1) + 1)

            units(-1, LEAD, UNITS + LEAD, now=False)
            with pool.Fori(0, NB - 1) as i:
                units(i, LEAD, UNITS + LEAD)
            units(NB - 1, LEAD, UNITS + 1, following=False)

        @block.scalar
        def _(act):
            act.preload_act_table_set(EXP_AND_LN)

            def finish_constants():
                act.wait_ge(setup_taken[1], 1)
                act.activation(neg_A[:], a_in[:], ACT.Exp).then_inc(act_step, 1)
                act.wait_ge(act_step, 1)
                act.mul(neg_A[:], neg_A[:], -1.0).then_inc(act_step, 1)
                act.mul(s_net[:, 0:1], s_in[:, 0:1], 4.0).then_inc(act_step, 1)
                act.mul(s_net[:, 1:2], s_in[:, 1:2], 2.0).then_inc(act_step, 1)
                act.mul(s_net[:, 2:3], s_in[:, 2:3], 1.0).then_inc(act_step, 1)
                act.wait_ge(act_step, 5)
                act.wait_ge(spread_built, 1)
                act.copy(spread[:].rearrange("p g m -> p (g m)"), a[:, 0, :]).then_inc(const_ready, 1)
                act.wait_ge(const_ready, 1)

            def decay(b, s):
                n = UNITS * b + s
                k = s % GROUPS
                after(act, d_rep_ready, n + 1)
                after(act, h_ready, n - (NA - 1 if s < NA - 1 else NA) + 1)
                act.activation(a[:, s % NA, :], d_rep[:], ACT.Exp,
                               scale=neg_A[:, s // GROUPS, group(k):group(k) + 1]).then_inc(a_ready, 1)

            def evacuate(b, step, arg, half, bank, use):
                after(act, work_full[bank], use + 1)
                src = work[bank]
                if step == "turn":
                    after(act, u_ready, 2 * b)
                    act.copy(xnT[:, cols(half)], src[:]).then_inc(xnT_ready, 1)
                elif step == "delta":
                    phase = 2 * b + arg
                    after(act, hi_ready[1], phase)
                    after(act, lo_ready[1], phase)
                    after(act, small_ready, phase)
                    act.activation(ez[:, cols(half)], src[:], ACT.Abs, bias=bias_dt[:, arg:arg + 1])
                    act.activation(pos[:, cols(half)], src[:], ACT.Relu, bias=bias_dt[:, arg:arg + 1])\
                        .then_inc(z_taken, 1)
                elif step == "B":
                    act.copy(B_rep[arg][:, cols(half)], src[:]).then_inc(B_ready, 1)
                elif step == "C":
                    act.copy(C_rep[arg][:, cols(half)], src[:]).then_inc(C_ready, 1)
                elif step == "net0":
                    act.activation(hidden[:, arg, :], src[:], ACT.Relu, scale=s_net[:, 0:1])
                    act.activation(h1_hi[:, arg, :], src[:], ACT.Relu, scale=s_net[:, 0:1]).then_inc(h1_ready, 1)
                elif step == "net1":
                    act.activation(hidden[:, arg, :], src[:], ACT.Relu, scale=s_net[:, 1:2]).then_inc(h2_ready, 1)
                elif step == "net2":
                    act.copy(gate[:, cols(half)], src[:]).then_inc(net_out, 1)

            def silu(b):
                after(act, net_out, HALVES * (b + 1))
                act.activation(gate[:], gate[:], ACT.Silu, scale=s_net[:, 2:3]).then_inc(gate_ready, 1)
                act.preload_act_table_set(EXP_AND_LN)

            def rough_rstd(b):
                after(act, moments_ready, b + 1)
                act.activation(rough[:], moments[:, :, 1], ACT.Ln, bias=eps[:, 0:1]).then_inc(log_var_ready, 1)
                after(act, log_var_ready, b + 1)
                act.activation(rough[:], rough[:], ACT.Exp, scale=-0.5).then_inc(rough_ready, 1)

            def normalise(b):
                after(act, newton_step, 4 * (b + 1))
                for j in range(TILES):
                    last = act.activation(x_in[:, j, :], x_in[:, j, :], ACT.Identity, scale=rstd[:, j:j + 1],
                                          bias=shift[:, j:j + 1])
                last.then_inc(xn_ready, 1)

            def exp_of(phase):
                after(act, z_taken, HALVES * (phase + 1))
                act.activation(ez[:], ez[:], ACT.Exp, scale=-1.0).then_inc(e_ready, 1)
                after(act, e_ready, phase + 1)
                after(act, log1p_ready, phase)
                act.activation(small[:], ez[:], ACT.Identity, scale=-0.5, bias=1.0).then_inc(slope_ready, 1)

            def log_of(phase):
                after(act, lo_ready[0], phase)
                after(act, u_ready, phase)
                act.activation(delta[:], ez[:], ACT.Ln, bias=1.0).then_inc(ln_ready, 1)

            def high(n, phase):
                after(act, delta_ready if n == 0 else u_ready, phase + 1)
                after(act, stacked[n], 64 * phase)
                act.copy(hi[n][:], (delta if n == 0 else pos)[:]).then_inc(hi_ready[n], 1)

            def units(i, sec, first, last, now=True, following=True):
                for s in range(first, last):
                    if (now and s + 1 < UNITS) or (following and s + 1 >= UNITS):
                        decay(*((i, s + 1) if s + 1 < UNITS else (i + 1, s + 1 - UNITS)))
                    for b, step, arg, half, bank, use in sec.results(s, i):
                        if step != "store":
                            evacuate(b, step, arg, half, bank, use)
                    if s == AT["silu"] and now:
                        silu(i)
                    if s == AT["rough_rstd"] and following:
                        rough_rstd(i + 1)
                        if not now:
                            act.wait_ge(small_loaded, 16 * 7)
                    if s == AT["normalise"] and following and now:
                        normalise(i + 1)
                    if s == AT["exp_0"] and following:
                        exp_of(2 * (i + 1))
                    if s == AT["log_0"] and following:
                        log_of(2 * (i + 1))
                        if not now:
                            finish_constants()
                    if s == AT["high_delta_0"] and following:
                        high(0, 2 * (i + 1))
                    if s == AT["high_u_0"] and following:
                        high(1, 2 * (i + 1))
                    if s == AT["exp_1"] and following:
                        exp_of(2 * (i + 1) + 1)
                    if s == AT["log_1"] and following:
                        log_of(2 * (i + 1) + 1)
                    if s == AT["high_delta_1"] and now:
                        high(0, 2 * i + 1)
                    if s == AT["high_u_1"] and now:
                        high(1, 2 * i + 1)

            units(-1, opening, LEAD, UNITS + LEAD, now=False)
            with act.Fori(0, NB - 1) as i:
                units(i, looped, LEAD, UNITS + LEAD)
            units(NB - 1, closing, LEAD, UNITS + LEAD, following=False)

        @block.vector
        def _(dve):
            dve.memset(eps[:], EPS).then_inc(dve_step, 1)
            def statistics(b):
                after(dve, x_loaded, 16 * (b + 1))
                for j in range(TILES):
                    last = dve.bn_stats(stats[:, j, :], x_in[:, j, :])
                last.then_inc(stats_ready, 1)

            def aggregate():
                for j in range(TILES):
                    last = dve.bn_aggr(moments[:, j, :], stats[:, j, :])
                last.then_inc(moments_ready, 1)

            def inverse(b):
                after(dve, rough_ready, b + 1)
                dve.scalar_tensor_tensor(out=newton[:], in0=moments[:, :, 1], scalar=EPS, in1=rough[:],
                                         op0=ALU.add, op1=ALU.mult).then_inc(newton_step, 1)
                after(dve, newton_step, 4 * b + 1)
                dve.scalar_tensor_tensor(out=newton[:], in0=newton[:], scalar=-0.5, in1=rough[:],
                                         op0=ALU.mult, op1=ALU.mult).then_inc(newton_step, 1)
                after(dve, newton_step, 4 * b + 2)
                dve.scalar_tensor_tensor(out=rstd[:], in0=newton[:], scalar=1.5, in1=rough[:],
                                         op0=ALU.add, op1=ALU.mult).then_inc(newton_step, 1)
                after(dve, newton_step, 4 * b + 3)
                dve.scalar_tensor_tensor(out=shift[:], in0=moments[:, :, 0], scalar=-1.0, in1=rstd[:],
                                         op0=ALU.mult, op1=ALU.mult).then_inc(newton_step, 1)

            def prepare_projections():
                dve.wait_ge(work_full[0], 1)
                for d in range(2):
                    for w, at in ((w_B, R), (w_C, R + S)):
                        src = work[0][:, d * (R + 2 * S) + at:d * (R + 2 * S) + at + S]
                        last = dve.tensor_copy(w[:, d, :].rearrange("p (c s) -> p c s", s=S),
                                               src.unsqueeze(1).to_broadcast([D, CH, S]))
                last.then_inc(setup_taken[0], 1)
                dve.wait_ge(work_full[1], 1)
                dve.tensor_copy(a_in[:].rearrange("p d g -> p (d g)"), work[1][:, 2 * D:2 * D + 2 * GROUPS])
                dve.tensor_copy(dtT[:].rearrange("r d m -> r (d m)"), work[1][0:R, 0:2 * D])\
                    .then_inc(setup_taken[1], 1)

            def normalise_first():
                dve.wait_ge(newton_step, 4)
                for j in range(TILES):
                    last = dve.tensor_scalar(x_in[:, j, :], x_in[:, j, :], rstd[:, j:j + 1], shift[:, j:j + 1],
                                             ALU.mult, ALU.add)
                last.then_inc(xn_ready, 1)

            def finish_weights():
                dve.wait_ge(work_full[0], 2)
                dve.tensor_copy(w_delta[:].rearrange("r d m -> r (d m)"), work[0][:, 0:2 * D])\
                    .then_inc(setup_taken[0], 1)
                dve.wait_ge(nets_loaded, 16 * 3)
                dve.tensor_tensor(w0[:], k0_in[:, 0, :], k0_in[:, 1, :], ALU.subtract).then_inc(dve_step, 1)
                dve.tensor_scalar(w1[:], k1_in, 2.0, -1.0, ALU.mult, ALU.add).then_inc(dve_step, 1)
                dve.tensor_scalar(w2[:], k2_in, 2.0, -1.0, ALU.mult, ALU.add).then_inc(dve_step, 1)
                dve.wait_ge(small_loaded, 16 * 7)
                dve.tensor_tensor(skips[:, 2:3], skips[:, 0:1], skips[:, 1:2], ALU.add).then_inc(dve_step, 1)
                dve.wait_ge(ident_ready, 1)
                dve.wait_ge(dve_step, 5)
                dve.tensor_scalar(skip_diag[:], ident[:], skips[:, 2:3], None, ALU.mult).then_inc(dve_step, 1)

            def first_softplus():
                dve.wait_ge(slope_ready, 1)
                dve.tensor_tensor(small[:], small[:], ez[:], ALU.mult).then_inc(small_ready, 1)
                log1p(0)
                dve.wait_ge(log1p_ready, 1)
                dve.tensor_tensor(delta[:], delta[:], pos[:], ALU.add).then_inc(delta_ready, 1)

            def log1p(phase):
                after(dve, ln_ready, phase + 1)
                after(dve, small_ready, phase + 1)
                dve.scalar_tensor_tensor(out=delta[:], in0=delta[:], scalar=-LOG_SLACK, in1=small[:],
                                         op0=ALU.add, op1=ALU.max).then_inc(log1p_ready, 1)

            def delta_times_x(b, phase):
                after(dve, delta_ready, phase + 1)
                after(dve, xnT_ready, HALVES * (b + 1))
                dve.tensor_tensor(pos[:], delta[:], xnT[:], ALU.mult).then_inc(u_ready, 1)

            def low(n, phase):
                after(dve, hi_ready[n], phase + 1)
                dve.tensor_tensor(lo[n][:], (delta if n == 0 else pos)[:], hi[n][:].bitcast(F32), ALU.subtract)\
                    .then_inc(lo_ready[n], 1)

            def input_term(b, s):
                n = UNITS * b + s
                after(dve, u_rep_ready, n + 1)
                if s % GROUPS == 0:
                    after(dve, B_ready, HALVES * (2 * b + s // GROUPS + 1))
                after(dve, ch_ready, n - NH + 1)
                dve.tensor_tensor(h[:, s % NH, :], u_rep[:], B_rep[s // GROUPS][:], ALU.mult).then_inc(bx_ready, 1)

            def scan(b, s):
                n = UNITS * b + s
                after(dve, bx_ready, n + 1)
                after(dve, a_ready, n + 1)
                t = slice(None) if s < GROUPS else slice(None, None, -1)
                dve.tensor_tensor_scan(h[:, s % NH, t], a[:, s % NA, t], h[:, s % NH, t], 0.0, ALU.mult, ALU.add)\
                    .then_inc(h_ready, 1)

            def low_h1(b, half):
                tiles = slice(GPSIMD_TILES[half], FM)
                after(dve, h1_ready, FM * (HALVES * b + half + 1))
                dve.tensor_tensor(h1_lo[:, tiles, :], hidden[:, tiles, :], h1_hi[:, tiles, :].bitcast(F32),
                                  ALU.subtract).then_inc(h1_lo_ready[1], 1)

            def gate_y(b):
                after(dve, summed, UNITS // QUADS * (b + 1))
                after(dve, gate_ready, b + 1)
                dve.tensor_tensor(gate[:], y[:], gate[:], ALU.mult).then_inc(gated_ready, 1)

            def add_residual(b, half, bank, use):
                after(dve, work_full[bank], use + 1)
                after(dve, moved, 16 * (1 + HALVES) * b + 16)
                dve.tensor_tensor(x_res[:, half * TH:(half + 1) * TH, :],
                                  work[bank][:].rearrange("p (j d) -> p j d", d=D),
                                  x_res[:, half * TH:(half + 1) * TH, :], ALU.add).then_inc(out_ready, 1)

            def units(i, sec, first, last, now=True, following=True):
                for s in range(first, last):
                    if s == AT["aggregate"] and following:
                        after(dve, stats_ready, i + 2)
                        after(dve, xn_ready, i + 1)
                    if (now and s < UNITS) or (following and s >= UNITS):
                        input_term(*((i, s) if s < UNITS else (i + 1, s - UNITS)))
                    if (now and s <= UNITS) or (following and s > UNITS):
                        scan(*((i, s - 1) if s <= UNITS else (i + 1, s - 1 - UNITS)))
                    if s == AT["statistics"] and following:
                        statistics(i + 1)
                    if s == AT["aggregate"] and following:
                        aggregate()
                        if not now:
                            prepare_projections()
                    if s == AT["inverse"] and following:
                        inverse(i + 1)
                        if not now:
                            normalise_first()
                            finish_weights()
                    if s == AT["log1p_0"] and following:
                        if now:
                            log1p(2 * (i + 1))
                        else:
                            first_softplus()
                    if s == AT["u_0"] and following:
                        delta_times_x(i + 1, 2 * (i + 1))
                    if s == AT["low_delta_0"] and following:
                        low(0, 2 * (i + 1))
                    if s == AT["low_u_0"] and following:
                        low(1, 2 * (i + 1))
                    if s == AT["low_h1_half1_vector"] and now:
                        low_h1(i, 1)
                    if s == AT["low_h1_half0_vector"] and following:
                        low_h1(i + 1, 0)
                    if s == AT["log1p_1"] and following:
                        log1p(2 * (i + 1) + 1)
                    if s == AT["u_1"] and now:
                        delta_times_x(i, 2 * i + 1)
                    if s == AT["low_delta_1"] and now:
                        low(0, 2 * i + 1)
                    if s == AT["low_u_1"] and now:
                        low(1, 2 * i + 1)
                    if s == AT["gate_y"] and now:
                        gate_y(i)
                    for b, step, arg, half, bank, use in sec.results(s, i):
                        if step == "store":
                            add_residual(b, half, bank, use)

            units(-1, opening, LEAD, UNITS + LEAD, now=False)
            with dve.Fori(0, NB - 1) as i:
                units(i, looped, LEAD, UNITS + LEAD)
            units(NB - 1, closing, LEAD, UNITS + LEAD, following=False)

        @block.tensor
        def _(pe):
            pe.wait_ge(proj_loaded, 16 * 6)
            pe.wait_ge(ident_ready, 1)
            W = R + 2 * S
            for d in range(2):
                last = pe.transpose(work[0][:, d * W:(d + 1) * W], xp_sb[:, d, :], ident[0:W, 0:W])
            last.then_inc(work_full[0], 1)
            for d in range(2):
                last = pe.transpose(work[1][0:R, d * D:(d + 1) * D], dt_sb[:, d, :], ident[:])
            for d in range(2):
                last = pe.transpose(work[1][:, 2 * D + d * GROUPS:2 * D + (d + 1) * GROUPS], a_nat[:, d, :],
                                    ident[0:GROUPS, 0:GROUPS])
            last.then_inc(work_full[1], 1)
            pe.wait_ge(setup_taken[0], 1)
            pe.wait_ge(setup_taken[1], 1)
            for d in range(2):
                last = pe.matmul(work[0][:, d * D:(d + 1) * D], xp_sb[0:R, d, :], dtT[:, d, :],
                                 start=True, stop=True)
            last.then_inc(work_full[0], 1)

            def selected(s):
                d, g = s // GROUPS, group(s % GROUPS)
                return d, g // (GROUPS // 2), spread[:, g % (GROUPS // 2), :]

            def replicate_delta(b, s):
                n = UNITS * b + s
                d, t, sel = selected(s)
                if s % GROUPS == 0:
                    after(pe, stacked[0], 64 * (2 * b + d + 1))
                after(pe, a_ready, n)
                for half in range(HALVES):
                    last = pe.matmul(d_rep[:, cols(half)], sel, stack[d][0][:, t, cols(half)],
                                     start=True, stop=True)
                last.then_inc(d_rep_ready, 1)

            def replicate_u(b, s):
                n = UNITS * b + s
                d, t, sel = selected(s)
                if s % GROUPS == 0:
                    after(pe, stacked[1], 64 * (2 * b + d + 1))
                after(pe, bx_ready, n)
                for half in range(HALVES):
                    last = pe.matmul(u_rep[:, cols(half)], sel, stack[d][1][:, t, cols(half)],
                                     start=True, stop=True)
                last.then_inc(u_rep_ready, 1)

            def sum_states(b, s):
                n = UNITS * b + s
                after(pe, ch_ready, n + 1)
                for half in range(HALVES):
                    for q in range(QUADS):
                        last = pe.matmul(y[q * Q:(q + 1) * Q, cols(half)], gather[:, (s % GROUPS) // QUADS, :],
                                         ch[:, (s - QUADS + 1 + q) % NCG, cols(half)], start=False,
                                         stop=(s == UNITS - 1), skip_group_check=True)
                last.then_inc(summed, 1)

            def skip_term(b):
                after(pe, gated_ready, b)
                for half in range(HALVES):
                    pe.matmul(y[:, cols(half)], skip_diag[:], xnT[:, cols(half)], start=True, stop=False,
                              skip_group_check=True)

            def bank_free(sec, i, p):
                if p >= 2:
                    after(pe, *taken(i, *sec.steps[p - 2]))
                elif sec is opening:
                    after(pe, setup_taken[(SETUP + p) % 2], 1 + p)
                else:
                    after(pe, *taken(i - 1, *body[p - 2]))

            def background(b, step, arg, half, bank, t):
                dst = work[bank]
                if step == "turn":
                    if half == 0:
                        after(pe, xn_ready, b + 1)
                    for j in range(TH):
                        last = pe.transpose(dst[:, j * P:(j + 1) * P], x_in[:, half * TH + j, :], ident[:])
                elif step in ("delta", "B", "C"):
                    if step == "delta" and arg == 0 and half == 0:
                        after(pe, xnT_ready, HALVES * (b + 1))
                    w = {"delta": w_delta, "B": w_B, "C": w_C}[step]
                    last = pe.matmul(dst[:], w[:, arg, :], xnT[:, cols(half)], start=True, stop=True)
                elif step == "net0":
                    last = pe.matmul(dst[:], w0[:, arg * P:(arg + 1) * P], xnT[:, cols(half)],
                                     start=True, stop=True)
                elif step == "net1":
                    if t == 0 and arg == 0:
                        for n in range(2):
                            after(pe, h1_lo_ready[n], HALVES * b + half + 1)
                    for part in (h1_hi, h1_lo):
                        last = pe.matmul(dst[:], w1[:, t, arg * P:(arg + 1) * P], part[:, t, :],
                                         start=(t == 0 and part is h1_hi), stop=(t == FM - 1 and part is h1_lo))
                    if t < FM - 1:
                        return
                elif step == "net2":
                    if t == 0:
                        after(pe, h2_ready, FM * (HALVES * b + half + 1))
                    last = pe.matmul(dst[:], w2[:, t, :], hidden[:, t, :], start=(t == 0), stop=(t == FM - 1))
                    if t < FM - 1:
                        return
                elif step == "store":
                    after(pe, gated_ready, b + 1)
                    for j in range(TH):
                        at = (half * TH + j) * P
                        last = pe.transpose(dst[:, j * P:(j + 1) * P], gate[:, at:at + P], ident[:])
                last.then_inc(work_full[bank], 1)

            def units(i, sec, first, last, now=True, following=True):
                for s in range(first, last):
                    if (now and s < UNITS) or (following and s >= UNITS):
                        replicate_u(*((i, s) if s < UNITS else (i + 1, s - UNITS)))
                    delta_next = (now and s + 1 < UNITS) or (following and s + 1 >= UNITS)
                    if delta_next and s not in LATE:
                        replicate_delta(*((i, s + 1) if s + 1 < UNITS else (i + 1, s + 1 - UNITS)))
                    if s % QUADS == 3 and (now and s - 4 < UNITS or following and s - 4 >= UNITS):
                        sum_states(*((i, s - 4) if s - 4 < UNITS else (i + 1, s - 4 - UNITS)))
                    if s == AT["skip_term"] and following:
                        skip_term(i + 1)
                    if s == FIRST_CONSTANTS and not now:
                        pe.wait_ge(dve_step, 6)
                        pe.wait_ge(const_ready, 1)
                        pe.wait_ge(gather_ready, 1)
                    for b, step, arg, half, bank, p, t in sec.parts(s, i):
                        if t == 0:
                            bank_free(sec, i, p)
                        background(b, step, arg, half, bank, t)
                    if delta_next and s in LATE:
                        replicate_delta(*((i, s + 1) if s + 1 < UNITS else (i + 1, s + 1 - UNITS)))

            units(-1, opening, LEAD, UNITS + LEAD, now=False)
            with pe.Fori(0, NB - 1) as i:
                units(i, looped, LEAD, UNITS + LEAD)
            units(NB - 1, closing, LEAD, UNITS + LEAD, following=False)


_PAIRS = ("x_proj", "dt_proj", "dt_bias", "A_log", "D_skip")


def kernel(**inputs):
    import numpy as np
    import concourse.bacc as bacc
    from concourse.bass_utils import run_bass_kernel_spmd

    a = {k: np.ascontiguousarray(v) for k, v in inputs.items()}
    arrays = {
        "x": a["L0_attn_x"],
        "x_proj0": a["L0_attn_x_proj_w"], "x_proj1": a["L0_attn_x_proj_b_w"],
        "dt_proj0": a["L0_attn_dt_proj_w"], "dt_proj1": a["L0_attn_dt_proj_b_w"],
        "dt_bias0": a["L0_attn_dt_proj_b"], "dt_bias1": a["L0_attn_dt_proj_b_b"],
        "A_log0": a["L0_attn_A_log"], "A_log1": a["L0_attn_A_b_log"],
        "D_skip0": a["L0_attn_D"], "D_skip1": a["L0_attn_D_b"],
        "k0": a["L0_ffn_k0"], "k1": a["L0_ffn_k1"],
        "k2": a["L0_ffn_k2"],
        "s0": a["L0_ffn_s0"].reshape(1, 1), "s1": a["L0_ffn_s1"].reshape(1, 1),
        "s2": a["L0_ffn_s2"].reshape(1, 1),
    }
    nc = bacc.Bacc("TRN2", target_bir_lowering=False, num_devices=1)
    ap = {n: nc.dram_tensor(f"in_{n}", v.shape, mybir.dt.from_np(v.dtype), kind="ExternalInput").ap()
          for n, v in arrays.items()}
    out = nc.dram_tensor("out", a["L0_attn_x"].shape, F32, kind="ExternalOutput").ap()
    pairs = [[ap[n + "0"], ap[n + "1"]] for n in _PAIRS]
    build_scan_and_gate(nc, ap["x"], *pairs, ap["k0"], ap["k1"], ap["k2"], [ap["s0"], ap["s1"], ap["s2"]], out)
    r = run_bass_kernel_spmd(nc, [{f"in_{n}": v for n, v in arrays.items()}], core_ids=[0])
    return r.results[0]["out"]
```
